# Optimizing a Trainium2 kernel written in Bass

```python
import numpy as np
import jax
import jax.numpy as jnp

def _softmax(x, axis=-1):
    return jax.nn.softmax(x, axis=axis)

def _gelu(x):
    return jax.nn.gelu(x, approximate=True)

def _silu(x):
    return jax.nn.silu(x)

def _sigmoid(x):
    return jax.nn.sigmoid(x)

def _layernorm(x, axis=-1, eps=1e-05):
    m = jnp.mean(x, axis=axis, keepdims=True)
    v = jnp.var(x, axis=axis, keepdims=True)
    return (x - m) / jnp.sqrt(v + eps)

def _scatter_add(tgt, idx, src, axis=0):
    return tgt.at[idx].add(src)

def _segment_sum(src, seg, n):
    return jax.ops.segment_sum(src, seg, n)
kernel_name = 'mk_decoder_postln_d1_seqx_r8_73bae4'

def setup_inputs(seed: int=0):
    np.random.seed(seed)
    _w = jnp.asarray

    def _rec_inputs():
        import jax
        import jax.numpy as jnp
        _rk = jax.random.key(seed)
        x = -0.000125 + 0.9999 * jax.random.normal(jax.random.fold_in(_rk, 1), (8, 56, 128), jnp.float32)
        _lenS = 56 - jax.random.randint(jax.random.fold_in(_rk, 7), (8,), 0, max(1, 56 // 4) + 1, jnp.int32)
        _lenS2 = 1500 - jax.random.randint(jax.random.fold_in(_rk, 8), (8,), 0, max(1, 1500 // 4) + 1, jnp.int32)
        _ctx_768P = jax.random.normal(jax.random.fold_in(_rk, 11), (8, 16, 96), jnp.float32)
        _ctx_768c = jax.random.dirichlet(jax.random.fold_in(_rk, 511), 0.3 * jnp.ones((16,), jnp.float32), (8, 1500))
        _ctx_768t = jnp.einsum('bsk,bkd->bsd', _ctx_768c, _ctx_768P)
        _ctx_768t = _ctx_768t * jax.lax.rsqrt(jnp.mean(jnp.square(_ctx_768t)) + 1e-12) * 0.953939
        ctx_768 = 0.00272024 + 0.999456 * (_ctx_768t + 0.3 * jax.random.normal(jax.random.fold_in(_rk, 611), (8, 1500, 96), jnp.float32))
        return (x, ctx_768)
    x, ctx_768 = _rec_inputs()

    def _L0_attn_setup():
        import jax, jax.numpy as jnp
        import numpy as np
        import math
        EPS = 1e-06
        H = 16

        def favorplus_features(x, proj, eps=EPS):
            xw = jnp.einsum('bhtd,hmd->bhtm', x, proj)
            xw = xw - jnp.max(xw, axis=-1, keepdims=True)
            exp_part = jnp.exp(xw)
            x_norm_sq = jnp.sum(x * x, axis=-1, keepdims=True)
            base = jnp.exp(-0.5 * x_norm_sq)
            return exp_part * base + eps
        key = jax.random.key(seed)
        ks = jax.random.split(key, 7)
        B, T, d = (4, 512, 128)
        h, m = (H, 32)
        dk = d // h
        s = 1.0 / math.sqrt(d)
        return {'x': jax.random.normal(ks[0], (B, T, d), jnp.float32), 'Wq': jax.random.normal(ks[1], (d, d), jnp.float32) * s, 'Wk': jax.random.normal(ks[2], (d, d), jnp.float32) * s, 'Wv': jax.random.normal(ks[3], (d, d), jnp.float32) * s, 'Wo': jax.random.normal(ks[4], (d, d), jnp.float32) * s, 'bo': jnp.zeros((d,), jnp.float32), 'proj': jax.random.normal(ks[5], (h, m, dk), jnp.float32)}
    _L0_attn_all = _L0_attn_setup()
    _L0_attn_in = {k: v for k, v in _L0_attn_all.items() if k in ('Wq', 'Wk', 'Wv', 'Wo', 'bo', 'proj')}
    del _L0_attn_all

    def _L0_xattn_setup():
        import jax, jax.numpy as jnp
        import numpy as np
        HEADS = 16
        DIM_HEAD = 64
        SCALE = DIM_HEAD ** (-0.5)
        QUERY_DIM = 128
        CONTEXT_DIM = 96
        INNER_DIM = HEADS * DIM_HEAD
        key = jax.random.key(seed)
        ks = jax.random.split(key, 7)
        B, Nq, Nk = (8, 512, 77)
        x = jax.random.normal(ks[0], (B, Nq, QUERY_DIM), dtype=jnp.float32)
        context = jax.random.normal(ks[1], (B, Nk, CONTEXT_DIM), dtype=jnp.float32)
        Wq = jax.random.normal(ks[2], (QUERY_DIM, INNER_DIM), dtype=jnp.float32) * QUERY_DIM ** (-0.5)
        Wk = jax.random.normal(ks[3], (CONTEXT_DIM, INNER_DIM), dtype=jnp.float32) * CONTEXT_DIM ** (-0.5)
        Wv = jax.random.normal(ks[4], (CONTEXT_DIM, INNER_DIM), dtype=jnp.float32) * CONTEXT_DIM ** (-0.5)
        Wo = jax.random.normal(ks[5], (INNER_DIM, QUERY_DIM), dtype=jnp.float32) * INNER_DIM ** (-0.5)
        bo = jnp.zeros((QUERY_DIM,), dtype=jnp.float32)
        return {'x': x, 'context': context, 'Wq': Wq, 'Wk': Wk, 'Wv': Wv, 'Wo': Wo, 'bo': bo}
    _L0_xattn_all = _L0_xattn_setup()
    _L0_xattn_in = {k: v for k, v in _L0_xattn_all.items() if k in ('Wq', 'Wk', 'Wv', 'Wo', 'bo')}
    del _L0_xattn_all

    def _L0_ffn_setup():
        import jax, jax.numpy as jnp
        import numpy as np
        DIM = 128
        HIDDEN = 384
        SCALE = 1.0 / 127.0

        def _dequant(w_int, dtype):
            return w_int.astype(dtype) * jnp.asarray(SCALE, dtype)
        key = jax.random.key(seed)
        k_x, k_g, k_u, k_d = jax.random.split(key, 4)
        x = jax.random.normal(k_x, (4, 256, DIM), dtype=jnp.float32)
        w_gate = jax.random.randint(k_g, (HIDDEN, DIM), -127, 128, dtype=jnp.int32)
        w_up = jax.random.randint(k_u, (HIDDEN, DIM), -127, 128, dtype=jnp.int32)
        w_down = jax.random.randint(k_d, (DIM, HIDDEN), -127, 128, dtype=jnp.int32)
        return {'x': x, 'w_gate': w_gate, 'w_up': w_up, 'w_down': w_down}
    _L0_ffn_all = _L0_ffn_setup()
    _L0_ffn_in = {k: v for k, v in _L0_ffn_all.items() if k in ('w_gate', 'w_up', 'w_down')}
    del _L0_ffn_all
    return {'x': x, 'ctx_768': ctx_768, 'L0_attn_Wq': _L0_attn_in['Wq'], 'L0_attn_Wk': _L0_attn_in['Wk'], 'L0_attn_Wv': _L0_attn_in['Wv'], 'L0_attn_Wo': _L0_attn_in['Wo'], 'L0_attn_bo': _L0_attn_in['bo'], 'L0_attn_proj': _L0_attn_in['proj'], 'L0_xattn_Wq': _L0_xattn_in['Wq'], 'L0_xattn_Wk': _L0_xattn_in['Wk'], 'L0_xattn_Wv': _L0_xattn_in['Wv'], 'L0_xattn_Wo': _L0_xattn_in['Wo'], 'L0_xattn_bo': _L0_xattn_in['bo'], 'L0_ffn_w_gate': _L0_ffn_in['w_gate'], 'L0_ffn_w_up': _L0_ffn_in['w_up'], 'L0_ffn_w_down': _L0_ffn_in['w_down']}

def reference(x, ctx_768, L0_attn_Wq, L0_attn_Wk, L0_attn_Wv, L0_attn_Wo, L0_attn_bo, L0_attn_proj, L0_xattn_Wq, L0_xattn_Wk, L0_xattn_Wv, L0_xattn_Wo, L0_xattn_bo, L0_ffn_w_gate, L0_ffn_w_up, L0_ffn_w_down):
    import jax
    import jax.numpy as jnp

    def _L0_attn_ref(x, Wq, Wk, Wv, Wo, bo, proj):
        import jax, jax.numpy as jnp
        import numpy as np
        import math
        EPS = 1e-06
        H = 16

        def favorplus_features(x, proj, eps=EPS):
            xw = jnp.einsum('bhtd,hmd->bhtm', x, proj)
            xw = xw - jnp.max(xw, axis=-1, keepdims=True)
            exp_part = jnp.exp(xw)
            x_norm_sq = jnp.sum(x * x, axis=-1, keepdims=True)
            base = jnp.exp(-0.5 * x_norm_sq)
            return exp_part * base + eps
        B, T, d = x.shape
        h = H
        dk = d // h
        m = proj.shape[1]

        def heads(W):
            return (x @ W.T).reshape(B, T, h, dk).transpose(0, 2, 1, 3)
        Q, K, V = (heads(Wq), heads(Wk), heads(Wv))
        scale = 1.0 / math.sqrt(dk)
        phiQ = favorplus_features(Q * scale, proj) / math.sqrt(m)
        phiK = favorplus_features(K * scale, proj) / math.sqrt(m)
        KV = jnp.einsum('bhtm,bhtd->bhmd', phiK, V)
        Ksum = jnp.sum(phiK, axis=2)
        num = jnp.einsum('bhtm,bhmd->bhtd', phiQ, KV)
        den = jnp.einsum('bhtm,bhm->bht', phiQ, Ksum)[..., None] + EPS
        out_heads = num / den
        merged = out_heads.transpose(0, 2, 1, 3).reshape(B, T, h * dk)
        return merged @ Wo.T + bo

    def _L0_xattn_ref(x, context, Wq, Wk, Wv, Wo, bo):
        import jax, jax.numpy as jnp
        import numpy as np
        HEADS = 16
        DIM_HEAD = 64
        SCALE = DIM_HEAD ** (-0.5)
        QUERY_DIM = 128
        CONTEXT_DIM = 96
        INNER_DIM = HEADS * DIM_HEAD
        B, Nq, _ = x.shape
        Nk = context.shape[1]
        q = x @ Wq
        k = context @ Wk
        v = context @ Wv
        q = q.reshape(B, Nq, HEADS, DIM_HEAD).transpose(0, 2, 1, 3)
        k = k.reshape(B, Nk, HEADS, DIM_HEAD).transpose(0, 2, 1, 3)
        v = v.reshape(B, Nk, HEADS, DIM_HEAD).transpose(0, 2, 1, 3)
        sim = jnp.einsum('bhid,bhjd->bhij', q, k) * SCALE
        attn = jax.nn.softmax(sim, axis=-1)
        out = jnp.einsum('bhij,bhjd->bhid', attn, v)
        out = out.transpose(0, 2, 1, 3).reshape(B, Nq, INNER_DIM)
        return out @ Wo + bo

    def _L0_ffn_ref(x, w_gate, w_up, w_down):
        import jax, jax.numpy as jnp
        import numpy as np
        DIM = 128
        HIDDEN = 384
        SCALE = 1.0 / 127.0

        def _dequant(w_int, dtype):
            return w_int.astype(dtype) * jnp.asarray(SCALE, dtype)
        wg = _dequant(w_gate, x.dtype)
        wu = _dequant(w_up, x.dtype)
        wd = _dequant(w_down, x.dtype)
        gate = jnp.einsum('bsd,hd->bsh', x, wg)
        up = jnp.einsum('bsd,hd->bsh', x, wu)
        h = jax.nn.silu(gate) * up
        return jnp.einsum('bsh,dh->bsd', h, wd)
    x = _layernorm(x + _L0_attn_ref(x, L0_attn_Wq, L0_attn_Wk, L0_attn_Wv, L0_attn_Wo, L0_attn_bo, L0_attn_proj), axis=-1)
    x = _layernorm(x + _L0_xattn_ref(x, ctx_768, L0_xattn_Wq, L0_xattn_Wk, L0_xattn_Wv, L0_xattn_Wo, L0_xattn_bo), axis=-1)
    x = _layernorm(x + _L0_ffn_ref(x, L0_ffn_w_gate, L0_ffn_w_up, L0_ffn_w_down), axis=-1)
    return x

_drawn_inputs = setup_inputs


def setup_inputs(seed=0):
    import zlib

    import numpy as np

    out = dict(_drawn_inputs(seed))
    spreads = {'L0_attn_bo': (0.0, 0.1), 'L0_xattn_bo': (0.0, 0.1)}
    factors = {}
    for name, (base, spread) in spreads.items():
        noise = np.random.default_rng([zlib.crc32(name.encode()), seed]).standard_normal(out[name].shape)
        drawn = base * np.exp(spread * noise) if base else spread * noise
        out[name] = jnp.asarray(drawn.astype(out[name].dtype))
    for name, factor in factors.items():
        out[name] = (out[name] * factor).astype(out[name].dtype)
    return out
```

```python
from contextlib import ExitStack

import concourse.bass as bass
from concourse import mybir

F32 = mybir.dt.float32
F32R = mybir.dt.float32r
I32 = mybir.dt.int32
ALU = mybir.AluOpType
ACT = mybir.ActivationFunctionType
AX = mybir.AxisListType

B, S, D = 8, 56, 128
SLOT = 64
PAIRS = B // 2
H = 16
DK = D // H
M = 32
G = 4
HG = H // G
KVW = HG * DK + HG
SELF_EPS = 1e-6
C, NCTX = 96, 1500
KT, KP = 12, 125
XD = 64
Q = H * S
QH = Q // 2
QT = Q // 128
KC = NCTX // 3
TU = 4
TW = NCTX // TU
HID = 384
HC = HID // 128
LN_EPS = 1e-5
SUM_P = 112

MAXES = [(j, c) for c in range(3) for j in range(QT)]


def ring_plan(prep, output):
    plan = {}
    if prep:
        for u, at in enumerate([(0, 1), (0, 3), (1, 1), (1, 3)]):
            plan[at] = ("transpose", u)
        places = [(t, p) for t in range(2, 7) for p in (1, 2, 3)] + [(t, p) for t in (7, 8, 9) for p in (1, 3)]
        for at, what in zip(places, MAXES):
            plan[at] = ("max", what)
        plan[(10, 0)] = ("maxrow", None)
    if output:
        plan[(6, 0)] = ("out", None)
        plan[(8, 0)] = ("x2T", None)
        plan[(9, 0)] = ("gate", None)
        plan[(10, 1)] = ("up", None)
        plan[(11, 0)] = ("down", None)
    return plan


PREP_SLOTS = 26
OUT_SLOTS = 6


def program(nc, x, ctx_in, sWq, sWk, sWv, sWo, sbo, proj, xWq, xWk, xWv, xWo, xbo, w_gate, w_up, w_down, out):
    with ExitStack() as stack:
        def sb(name, shape, dt=F32):
            return stack.enter_context(nc.sbuf_tensor(name, shape, dt))

        def ps(name, shape):
            return stack.enter_context(nc.psum_tensor(name, shape, F32))

        def sem(name):
            return stack.enter_context(nc.semaphore(name))

        ident = sb("ident", [128, 128])
        block_mask = sb("block_mask", [128, KVW])
        half_norm = sb("half_norm", [128, H])
        minus_half = sb("minus_half", [128, PAIRS])
        wT_self = sb("wT_self", [128, 4, 128])
        proj_sb = sb("proj_sb", [128, G, DK])
        sbo_sb = sb("sbo_sb", [128, D])
        xbo_sb = sb("xbo_sb", [128, D])
        wqk = sb("wqk", [128, H, C])
        wvo = sb("wvo", [C, H, D])
        ffn_int = sb("ffn_int", [128, 3, HC, 128], I32)
        ffn_nat = sb("ffn_nat", [128, 3, HC, 128])
        ffnT = sb("ffnT", [128, 3, HC, 128])

        x_sb = sb("x_sb", [128, PAIRS, D])
        half_sq = sb("half_sq", [128, 2, PAIRS, H])
        feat_max = sb("feat_max", [128, 2, PAIRS, H])
        feat_shift = sb("feat_shift", [128, 2, PAIRS, H])
        den = sb("den", [128, PAIRS, G, HG])
        rden = sb("rden", [128, PAIRS, G, HG])
        merged = sb("merged", [128, PAIRS, D])
        mergedT = sb("mergedT", [128, PAIRS, D])
        y1 = sb("y1", [128, PAIRS, D])
        stats1 = sb("stats1", [128, PAIRS, 6])
        mv1 = sb("mv1", [128, PAIRS, 2])
        ve1 = sb("ve1", [128, PAIRS])
        rstd1 = sb("rstd1", [128, PAIRS])
        x1 = sb("x1", [128, PAIRS, D])
        x1b = sb("x1b", [128, PAIRS, D])
        x1T = sb("x1T", [128, 512])

        q_all = sb("q_all", [C, B, Q])
        ctx_nat = sb("ctx_nat", [KP, 2, KT, C])
        cn_hi = [sb("cn_hi0", [KP, KT, C + 1], F32R)]
        cn_lo = [sb("cn_lo0", [KP, KT, C + 1], F32R)]
        ct_hi = [sb("ct_hi0", [C + 1, NCTX], F32R)]
        ct_lo = [sb("ct_lo0", [C, NCTX], F32R)]
        q_hi = [sb("q_hi0", [C + 1, Q], F32R)]
        q_lo = [sb("q_lo0", [C, Q], F32R)]
        max_part = sb("max_part", [128, QT, 3])
        max_neg = sb("max_neg", [128, QT])
        max_row = sb("max_row", [QT, 128], F32R)
        sums = sb("sums", [SUM_P, Q // SUM_P])
        rsums = sb("rsums", [SUM_P, Q // SUM_P])
        u_norm = sb("u_norm", [C, H, 2, SLOT])

        stats2 = sb("stats2", [128, 6])
        mv2 = sb("mv2", [128, 2])
        ve2 = sb("ve2", [128, 1])
        rstd2 = sb("rstd2", [128, 1])
        x3 = sb("x3", [128, PAIRS, D])

        setup_only = ExitStack()

        def early(name, shape, dt=F32):
            return setup_only.enter_context(nc.sbuf_tensor(name, shape, dt))

        w_self = early("w_self", [128, 4, 128])
        proj_wide = early("proj_wide", [128, G, H, DK])
        projT = early("projT", [128, 512])
        kq_scaled = early("kq_scaled", [128, 2, 512])
        kq_sq = early("kq_sq", [128, 2, 512])
        v_masked = early("v_masked", [128, PAIRS, 2, G, KVW])
        phi = early("phi", [128, 2, PAIRS, H, M])
        kv = early("kv", [128, PAIRS, G, 2, KVW])
        phiqT = early("phiqT", [128, PAIRS, G, 128])
        wq_nat = early("wq_nat", [128, H * XD])
        wk_nat = early("wk_nat", [C, H * XD])
        wv_nat = early("wv_nat", [C, H * XD])
        wo_nat = early("wo_nat", [128, 8, D])
        wqT = early("wqT", [128, 8, D])
        wkT = early("wkT", [128, 8, C])
        wvT = early("wvT", [128, 8, C])
        xT = early("xT", [128, 512])
        setup_only.close()
        for pair_of, name, shape in (
                (cn_hi, "cn_hi1", [KP, KT, C + 1]), (cn_lo, "cn_lo1", [KP, KT, C + 1]), (ct_hi, "ct_hi1", [C + 1, NCTX]),
                (ct_lo, "ct_lo1", [C, NCTX]), (q_hi, "q_hi1", [C + 1, Q]), (q_lo, "q_lo1", [C, Q])):
            pair_of.append(sb(name, shape, F32R))
        p_full = [sb(f"p_full{i}", [KP, Q]) for i in range(2)]
        p_hi = [sb(f"p_hi{i}", [KP, Q], F32R) for i in range(3)]
        p_lo = [sb(f"p_lo{i}", [KP, Q], F32R) for i in range(3)]
        u = sb("u", [C + 1, Q])
        rsum_row = sb("rsum_row", [1, Q])
        rsum_all = sb("rsum_all", [C, Q])
        y2 = sb("y2", [128, D])
        x2 = sb("x2", [128, D])
        x2T = sb("x2T", [128, 128])
        tanh_g = sb("tanh_g", [128, HID])
        silu_g = sb("silu_g", [128, HID])
        hidT = sb("hidT", [128, HC, 128])

        sc = [ps(f"sc{i}", [128, 2, 512]) for i in range(2)]
        acc = ps("acc", [128, 2, 512])
        mx = [ps(f"mx{i}", [128, 512]) for i in range(2)]
        banks = [sc[0][:, 0, :], sc[0][:, 1, :], sc[1][:, 0, :], sc[1][:, 1, :],
                 acc[:, 0, :], acc[:, 1, :], mx[0][:, :], mx[1][:, :]]

        PR = range(PAIRS)
        XW = [(n, j) for n in (0, 1) for j in PR]
        WT = [("q", 0), ("k", 0), ("q", 1), ("k", 1)]
        WV = [("v", 0), ("v", 1)]
        AB = [(i, par) for i in range(2) for par in range(2)]
        FILLS = ([("xT", "act"), ("wT", "dve"), ("projT", "act"), ("kT", "dve"), ("qT", "dve"), ("v", "act"),
                  ("norm", "dve")]
                 + [(("xw", n), "dve") for n in XW[:4]]
                 + [(("wT", n), "act") for n in WT]
                 + [(("xw", n), "dve") for n in XW[4:]]
                 + [(("wqk", n), "act") for n in AB]
                 + [(("kv", j), "dve") for j in PR]
                 + [(("phiqT", j), "act") for j in PR]
                 + [(("num", j), "dve") for j in PR]
                 + [(("wT", n), "act") for n in WV]
                 + [(("ffnT", i), "act") for i in range(3)]
                 + [(("wvo", n), "act") for n in AB]
                 + [(("mergedT", j), "act") for j in PR]
                 + [(("self", j), "dve") for j in PR]
                 + [(("x1T", j), "act") for j in PR]
                 + [(("qk", h), "act" if h % 2 else "dve") for h in range(H)])
        FILL_AT = {name: i for i, (name, _) in enumerate(FILLS)}

        ACT_SETUP = (["xT", "projT", "v0", "v"]
                     + ["square0", "square1"]
                     + [("exp", n) for n in XW[:4]] + [("wT", n) for n in WT]
                     + [("exp", n) for n in XW[4:]] + [("wqk", n) for n in AB]
                     + [("phiqT", j) for j in PR]
                     + [("wT", n) for n in WV] + [("ffnT", i) for i in range(3)] + [("wvo", n) for n in AB]
                     + [("mergedT", j) for j in PR] + [("x1T", j) for j in PR]
                     + [("qk", h) for h in range(1, H, 2)])
        DVE_SETUP = (["wT", "kT", "qT", "norm"]
                     + [s for n in XW[:4] for s in (("fmax", n), ("shift", n), ("xw", n))]
                     + [("eps", n) for n in XW[:4]]
                     + [s for n in XW[4:] for s in (("fmax", n), ("shift", n), ("xw", n))]
                     + [("eps", n) for n in XW[4:]]
                     + [("kv", j) for j in PR]
                     + [s for j in PR for s in (("den0", j), ("den", j), ("rden", j), ("num0", j), ("num", j))]
                     + [("ffn", i) for i in range(3)]
                     + ["xbias"]
                     + [s for j in PR for s in (("self", j), ("stats", j), ("aggr", j))]
                     + ["ve"] + [("x1", j) for j in PR] + ["x1b"]
                     + [("qk", h) for h in range(0, H, 2)])
        POOL_SETUP = (["x_zero", "ident0", "ident", "wide_zero", "norm0", "norm1", "norm2", "mask0", "v_zero",
                       "minus_half"] + [("wide", hl) for hl in range(HG)] + [("mask", hl) for hl in range(HG)]
                      + [("ones", 0), ("ones", 1), "unorm_zero", "ones_nat0", "ones0", "rstd", "ones_nat1", "ones1"])
        setup = {"act": sem("act_setup"), "dve": sem("dve_setup"), "pool": sem("pool_setup"), "pe": sem("pe_setup")}
        ORDER = {"act": ACT_SETUP, "dve": DVE_SETUP, "pool": POOL_SETUP, "pe": [n for n, _ in FILLS]}
        COUNT = {e: {n: i + 1 for i, n in enumerate(names)} for e, names in ORDER.items()}
        said = {e: 0 for e in ORDER}

        def done(engine, ins, name):
            assert ORDER[engine][said[engine]] == name, (engine, name, ORDER[engine][said[engine]])
            said[engine] += 1
            ins.then_inc(setup[engine], 1)

        def after(eng, engine, name):
            eng.wait_ge(setup[engine], COUNT[engine][name])

        x_landed = sem("x_landed")
        self_landed = sem("self_landed")
        proj_landed = sem("proj_landed")
        bias_landed = sem("bias_landed")
        xw_landed = sem("xw_landed")
        ffn_landed = sem("ffn_landed")
        ctx_landed = [sem(f"ctx_landed{i}") for i in range(2)]
        scores_ready = sem("scores_ready")
        phi_ready = sem("phi_ready")
        plo_ready = sem("plo_ready")
        p_ready = sem("p_ready")
        pv_done = sem("pv_done")
        u_ready = sem("u_ready")
        mx_filled = sem("mx_filled")
        mx_freed = sem("mx_freed")
        cthi_ready = sem("cthi_ready")
        qhi_ready = sem("qhi_ready")
        qlo_ready = sem("qlo_ready")
        nathi_ready = sem("nathi_ready")
        nat_ready = sem("nat_ready")
        maxneg_ready = sem("maxneg_ready")
        maxrow_ready = sem("maxrow_ready")
        maxrow_landed = sem("maxrow_landed")
        sums_landed = sem("sums_landed")
        rsums_ready = sem("rsums_ready")
        rrow_landed = sem("rrow_landed")
        rall_ready = sem("rall_ready")
        unorm_ready = sem("unorm_ready")
        out_steps = sem("out_steps")
        rstd_ready = sem("rstd_ready")
        tanh_ready = sem("tanh_ready")
        stored = sem("stored")

        OUT_STEPS = ["y2", "stats", "aggr", "ve", "x2", "x2T", "silu", "hid", "y3", "stats3", "aggr3", "ve3", "x3"]

        def out_step(pair, name):
            return len(OUT_STEPS) * pair + OUT_STEPS.index(name) + 1

        def ring_base(b, par):
            pairs_out = 0 if isinstance(b, int) and b == 0 else None
            if pairs_out is None:
                if isinstance(b, int):
                    pairs_out = (b - 1) // 2
                    return PREP_SLOTS * (b + 1) + OUT_SLOTS * pairs_out
                k = b[1]
                return PREP_SLOTS * (2 * k + (1 if par else 2)) + PREP_SLOTS + OUT_SLOTS * k
            return PREP_SLOTS

        block = stack.enter_context(nc.Block())

        def slots(plan):
            n, number = 0, {}
            for at in sorted(plan):
                number[at] = n
                n += 2 if plan[at][0] == "down" else 1
            return number

        def sequence_loop(eng, work):
            work(0, 0, PREP_SLOTS, True, None)
            with eng.Fori(0, 3) as k:
                per = 2 * PREP_SLOTS + OUT_SLOTS
                work(2 * k + 1, 1, per * k + 2 * PREP_SLOTS, True, None)
                work(2 * k + 2, 0, per * k + 3 * PREP_SLOTS, True, k)
            work(B - 1, 1, 3 * (2 * PREP_SLOTS + OUT_SLOTS) + 2 * PREP_SLOTS, False, None)

        LAST_BASE = 3 * (2 * PREP_SLOTS + OUT_SLOTS) + 2 * PREP_SLOTS
        FINAL = ["out", "x2T", "gate", "up", "down"]

        def wait(eng, s, value):
            if isinstance(value, int) and value <= 0:
                return
            eng.wait_ge(s, value)

        pool_waited = sem("pool_waited")
        dve_waited = sem("dve_waited")

        @block.sync
        def _(sp):
            after(sp, "pool", "x_zero")
            for par in range(2):
                sp.dma_start(x_sb[SLOT * par:SLOT * par + S, :, :],
                             x.rearrange("(j p) i d -> p i j d", p=2)[par]).then_inc(x_landed, 16)
            for n, w in enumerate((sWq, sWk, sWv, sWo)):
                sp.dma_start(w_self[:, n, :], w).then_inc(self_landed, 16)
            sp.dma_start(proj_sb[:], proj.rearrange("(g h) m d -> (h m) g d", g=G)).then_inc(proj_landed, 16)
            for b in range(2):
                sp.dma_start(ctx_nat[:, b], ctx_in[b].rearrange("(p t) c -> p t c", t=KT)).then_inc(ctx_landed[b], 16)
            for dst, bias in ((sbo_sb, sbo), (xbo_sb, xbo)):
                sp.dma_start(dst[:], bias.rearrange("(a d) -> a d", a=1).broadcast_to([128, D])).then_inc(bias_landed, 16)

            def place_maxima(par):
                sp.dma_start(q_hi[par][C:C + 1, :].rearrange("a (j q) -> a j q", j=QT).bitcast(F32),
                             max_row[:, :].bitcast(F32)).then_inc(maxrow_landed, 16)

            def work(b, par, load):
                if load:
                    wait(sp, cthi_ready, TU * (b + 1))
                    wait(sp, nat_ready, b + 1)
                    src = ctx_in[b + 2].rearrange("(p t) c -> p t c", t=KT)
                    sp.dma_start(ctx_nat[:, par], src).then_inc(ctx_landed[par], 16)
                if not (isinstance(b, int) and b == B - 1):
                    sp.wait_ge(maxrow_ready, b + 2)
                    place_maxima(1 - par)
                sp.wait_ge(u_ready, b + 1)
                sp.dma_start(sums[:], u[C:C + 1, :].rearrange("a (p n) -> a p n", p=SUM_P)).then_inc(sums_landed, 16)
                sp.wait_ge(rsums_ready, b + 1)
                sp.dma_start(rsum_row[0:1, :].rearrange("a (p n) -> a p n", p=SUM_P), rsums[:]).then_inc(rrow_landed, 16)

            sp.wait_ge(maxrow_ready, 1)
            place_maxima(0)
            with sp.Fori(0, 3) as k:
                work(2 * k, 0, True)
                work(2 * k + 1, 1, True)
            work(B - 2, 0, False)
            work(B - 1, 1, False)
            sp.wait_ge(out_steps, out_step(PAIRS - 1, "x3"))
            for par in range(2):
                sp.dma_start(out.rearrange("(j p) i d -> p i j d", p=2)[par],
                             x3[SLOT * par:SLOT * par + S, :, :]).then_inc(stored, 16)
            sp.wait_ge(stored, 32)

        @block.gpsimd
        def _(pool):
            done("pool", pool.memset(x_sb[:], 0.0), "x_zero")
            done("pool", pool.memset(ident[:], 0.0), "ident0")
            after(pool, "pool", "ident0")
            done("pool", pool.affine_select(out=ident[:], in_=ident[:], compare_op=ALU.not_equal, fill=1.0, base=0,
                                            pattern=[[-1, 128]], channel_multiplier=1), "ident")
            done("pool", pool.memset(proj_wide[:], 0.0), "wide_zero")
            done("pool", pool.memset(half_norm[:], 0.5), "norm0")
            after(pool, "pool", "norm0")
            done("pool", pool.affine_select(out=half_norm[:], in_=half_norm[:], compare_op=ALU.is_ge, fill=0.0, base=0,
                                            pattern=[[-DK, H]], channel_multiplier=1), "norm1")
            after(pool, "pool", "norm1")
            done("pool", pool.affine_select(out=half_norm[:], in_=half_norm[:], compare_op=ALU.is_ge, fill=0.0, base=DK - 1,
                                            pattern=[[DK, H]], channel_multiplier=-1), "norm2")
            done("pool", pool.memset(block_mask[:], 0.0), "mask0")
            done("pool", pool.memset(v_masked[:], 0.0), "v_zero")
            done("pool", pool.memset(minus_half[:], -0.5), "minus_half")
            pool.wait_ge(proj_landed, 16)
            for hl in range(HG):
                rows = slice(M * hl, M * hl + M)
                after(pool, "pool", ("wide", hl - 1) if hl else "minus_half")
                for g in range(G):
                    last = pool.tensor_copy(proj_wide[rows, g, HG * g + hl, :], proj_sb[rows, g, :])
                done("pool", last, ("wide", hl))
            for hl in range(HG):
                rows = slice(M * hl, M * hl + M)
                after(pool, "pool", ("mask", hl - 1) if hl else ("wide", HG - 1))
                pool.memset(block_mask[rows, DK * hl:DK * hl + DK], 1.0)
                done("pool", pool.memset(block_mask[rows, HG * DK + hl:HG * DK + hl + 1], 1.0), ("mask", hl))
            for par in range(2):
                after(pool, "pool", ("ones", par - 1) if par else ("mask", HG - 1))
                for j in PR:
                    last = pool.memset(v_masked[SLOT * par:SLOT * par + S, j, par, :, HG * DK:], 1.0)
                done("pool", last, ("ones", par))
            after(pool, "pool", ("ones", 1))
            done("pool", pool.memset(u_norm[:], 0.0), "unorm_zero")
            pool.memset(cn_hi[0][:, :, C:C + 1].bitcast(F32), 1.0)
            done("pool", pool.memset(cn_lo[0][:, :, C:C + 1].bitcast(F32), 0.0), "ones_nat0")
            after(pool, "pool", "ones_nat0")
            done("pool", pool.memset(ct_hi[0][C:C + 1, :].bitcast(F32), 1.0), "ones0")
            after(pool, "pool", "ones0")
            after(pool, "dve", "ve")
            done("pool", pool.tensor_tensor(rstd1[:], ve1[:], minus_half[:], ALU.pow), "rstd")

            def split_queries(b, par):
                wait(pool, scores_ready, KT * (b - 1))
                pool.sem_inc(pool_waited, 1)
                pool.tensor_copy(q_hi[par][0:C, :], q_all[:, b, :]).then_inc(qhi_ready, 1)
                pool.wait_ge(qhi_ready, b + 1)
                pool.sem_inc(pool_waited, 1)
                pool.tensor_tensor(q_lo[par][:], q_all[:, b, :], q_hi[par][0:C, :].bitcast(F32),
                                   ALU.subtract).then_inc(qlo_ready, 1)

            def split_context(b, par):
                pool.wait_ge(ctx_landed[par], 16 * landing(b, par))
                wait(pool, pv_done, KT * (b - 1))
                pool.wait_ge(qlo_ready, b + 1)
                pool.sem_inc(pool_waited, 1)
                pool.tensor_copy(cn_hi[par][:, :, 0:C], ctx_nat[:, par]).then_inc(nathi_ready, 1)
                pool.wait_ge(nathi_ready, b + 1)
                pool.sem_inc(pool_waited, 1)
                pool.tensor_tensor(cn_lo[par][:, :, 0:C], ctx_nat[:, par], cn_hi[par][:, :, 0:C].bitcast(F32),
                                   ALU.subtract).then_inc(nat_ready, 1)

            def normalize(b, par):
                pool.wait_ge(rrow_landed, 16 * (b + 1))
                wait(pool, nat_ready, b + 2 if not (isinstance(b, int) and b >= B - 2) else B)
                pool.sem_inc(pool_waited, 1)
                pool.partition_broadcast(rsum_all[:], rsum_row[0:1, :], C).then_inc(rall_ready, 1)
                pool.wait_ge(rall_ready, b + 1)
                pool.sem_inc(pool_waited, 1)
                pool.tensor_tensor(u_norm[:, :, par, 0:S], u[0:C, :].rearrange("c (h i) -> c h i", h=H),
                                   rsum_all[:].rearrange("c (h i) -> c h i", h=H), ALU.mult).then_inc(unorm_ready, 1)

            def rstd(pair, n, step):
                pool.wait_ge(out_steps, out_step(pair, step))
                pool.tensor_tensor(rstd2[:], ve2[:], minus_half[:, 0:1], ALU.pow).then_inc(rstd_ready, 1)

            def landing(b, par):
                if isinstance(b, int):
                    return b // 2 + 1
                return landing_of[0]

            landing_of = [None]
            after(pool, "pool", "rstd")
            after(pool, "dve", ("qk", H - 2))
            after(pool, "act", ("qk", H - 1))
            split_queries(0, 0)
            split_context(0, 0)
            pool.memset(cn_hi[1][:, :, C:C + 1].bitcast(F32), 1.0)
            done("pool", pool.memset(cn_lo[1][:, :, C:C + 1].bitcast(F32), 0.0), "ones_nat1")
            after(pool, "pool", "ones_nat1")
            pool.wait_ge(nat_ready, 1)
            done("pool", pool.memset(ct_hi[1][C:C + 1, :].bitcast(F32), 1.0), "ones1")
            after(pool, "pool", "ones1")
            split_queries(1, 1)
            split_context(1, 1)
            with pool.Fori(0, 3) as k:
                landing_of[0] = k + 2
                pool.wait_ge(unorm_ready, 0 + 2 * k) if False else None
                split_queries(2 * k + 2, 0)
                split_context(2 * k + 2, 0)
                normalize(2 * k, 0)
                split_queries(2 * k + 3, 1)
                split_context(2 * k + 3, 1)
                normalize(2 * k + 1, 1)
                rstd(k, 0, "ve")
                rstd(k, 1, "ve3")
            normalize(B - 2, 0)
            normalize(B - 1, 1)
            rstd(PAIRS - 1, 0, "ve")
            rstd(PAIRS - 1, 1, "ve3")

        @block.scalar
        def _(act):
            act.dma_start(wq_nat[:], xWq).then_inc(xw_landed, 16)
            act.dma_start(wk_nat[:], xWk).then_inc(xw_landed, 16)
            act.dma_start(wv_nat[:], xWv).then_inc(xw_landed, 16)
            act.dma_start(wo_nat[:], xWo.rearrange("(n p) d -> p n d", p=128)).then_inc(xw_landed, 16)
            act.dma_start(ffn_int[:, 0], w_gate.rearrange("(c p) d -> p c d", p=128)).then_inc(ffn_landed, 16)
            act.dma_start(ffn_int[:, 1], w_up.rearrange("(c p) d -> p c d", p=128)).then_inc(ffn_landed, 16)
            act.dma_start(ffn_int[:, 2], w_down.rearrange("p (c h) -> p c h", c=HC)).then_inc(ffn_landed, 16)

            def evacuate(dst, name, src, step=None, scale=1.0):
                after(act, "pe", name)
                done("act", act.activation(dst, src, ACT.Copy, scale=scale), step or name)

            def bank(name):
                return banks[FILL_AT[name] % 8]

            evacuate(xT[:], "xT", bank("xT"))
            evacuate(projT[:], "projT", bank("projT"))
            after(act, "pool", ("ones", 1))
            for par in range(2):
                rows = slice(SLOT * par, SLOT * par + S)
                src = bank("v").rearrange("p (j g c) -> p j g c", j=PAIRS, g=G)[rows]
                evacuate(v_masked[rows, :, par, :, 0:HG * DK], "v", src, "v" if par else "v0")
            for n, step in enumerate(("kT", "qT")):
                after(act, "dve", step)
                done("act", act.activation(kq_sq[:, n], kq_scaled[:, n], ACT.Square), f"square{n}")

            def exp_features(n, j):
                after(act, "dve", ("xw", (n, j)))
                done("act", act.activation(phi[:, n, j], phi[:, n, j], ACT.Exp), ("exp", (n, j)))

            def weight_copy(w, i):
                dst = {"q": wqT, "k": wkT, "v": wvT}[w]
                width = D if w == "q" else C
                src = bank(("wT", (w, i)))[:, 0:4 * width].rearrange("p (n c) -> p n c", n=4)
                evacuate(dst[:, 4 * i:4 * i + 4, :], ("wT", (w, i)), src)

            for n in XW[:4]:
                exp_features(*n)
            for n in WT:
                weight_copy(*n)
            for n in XW[4:]:
                exp_features(*n)
            for i, par in AB:
                dst = wqk[:, 8 * i:8 * i + 8, :].rearrange("p (n two) c -> p two n c", two=2)[:, par]
                src = bank(("wqk", (i, par)))[:, 0:4 * C].rearrange("p (n c) -> p n c", n=4)
                evacuate(dst, ("wqk", (i, par)), src, scale=float(XD) ** -0.5)
            for j in PR:
                evacuate(phiqT[:, j], ("phiqT", j), bank(("phiqT", j)).rearrange("p (g s) -> p g s", g=G))
            for n in WV:
                weight_copy(*n)
            for i in range(3):
                src = bank(("ffnT", i))[:, 0:HID].rearrange("p (c n) -> p c n", c=HC)
                evacuate(ffnT[:, i], ("ffnT", i), src)
            for i, par in AB:
                dst = wvo[:, 8 * i:8 * i + 8, :].rearrange("p (n two) d -> p two n d", two=2)[:, par]
                src = bank(("wvo", (i, par)))[0:C, :].rearrange("p (n d) -> p n d", n=4)
                evacuate(dst, ("wvo", (i, par)), src)
            for j in PR:
                evacuate(mergedT[:, j], ("mergedT", j), bank(("mergedT", j))[:, 0:128])
            for j in PR:
                evacuate(x1T[:, 128 * j:128 * j + 128], ("x1T", j), bank(("x1T", j))[:, 0:128])
            for h in range(1, H, 2):
                src = bank(("qk", h))[0:C, :].rearrange("c (b s) -> c b s", b=B)[:, :, 0:S]
                evacuate(q_all[:].rearrange("c b (h i) -> c b h i", h=H)[:, :, h, :], ("qk", h), src)

            def context_hi(b, par, slot, unit):
                act.wait_ge(mx_filled, slot + 1)
                act.activation(ct_hi[par][0:C, TW * unit:TW * unit + TW], mx[unit % 2][0:C, 0:TW],
                               ACT.Copy).then_inc(cthi_ready, 1)

            def collect(b):
                act.wait_ge(pv_done, KT * (b + 1))
                wait(act, unorm_ready, b)
                act.activation(u[:].rearrange("c (s q) -> c s q", s=2), acc[0:C + 1, :, 0:QH],
                               ACT.Copy).then_inc(u_ready, 1)

            def tanh(pair, slot, at):
                act.wait_ge(mx_filled, slot + 1)
                act.activation(tanh_g[:], mx[at % 2][:, 0:HID], ACT.Tanh, scale=0.5).then_inc(tanh_ready, 1)

            def work(b, par, base, prep, pair):
                plan = ring_plan(prep, pair is not None)
                number = slots(plan)
                for t in range(KT):
                    g = KT * b + t
                    act.wait_ge(scores_ready, g + 1)
                    wait(act, plo_ready, g - 1)
                    act.activation(p_full[t % 2][:].rearrange("k (s q) -> k s q", s=2), sc[t % 2][0:KP, :, 0:QH],
                                   ACT.Exp).then_inc(p_ready, 1)
                    wait(act, pv_done, g - 2)
                    act.activation(p_hi[t % 3][:].rearrange("k (s q) -> k s q", s=2), sc[t % 2][0:KP, :, 0:QH],
                                   ACT.Exp).then_inc(phi_ready, 1)
                    for p in range(4):
                        what = plan.get((t, p))
                        if what and what[0] == "transpose":
                            context_hi(b + 1, 1 - par, base + number[(t, p)], what[1])
                        if what and what[0] == "gate":
                            tanh(pair, base + number[(t, p)], number[(t, p)])
                    if t == 1 and not (isinstance(b, int) and b == 0):
                        collect(b - 1)

            for unit in range(TU):
                context_hi(0, 0, unit, unit)
            sequence_loop(act, work)
            collect(B - 1)
            tanh(PAIRS - 1, LAST_BASE + FINAL.index("gate"), FINAL.index("gate"))

        @block.vector
        def _(dve):
            def bank(name):
                return banks[FILL_AT[name] % 8]

            after(dve, "pe", "wT")
            done("dve", dve.tensor_copy(wT_self[:], bank("wT").rearrange("p (n d) -> p n d", n=4)), "wT")
            for n, name in enumerate(("kT", "qT")):
                after(dve, "pe", name)
                done("dve", dve.tensor_scalar(kq_scaled[:, n], bank(name), float(DK) ** -0.5, None, ALU.mult), name)

            def features(n, j):
                name = ("xw", (n, j))
                after(dve, "pe", name)
                xw = bank(name).rearrange("p (h m) -> p h m", h=H)
                done("dve", dve.tensor_reduce(feat_max[:, n, j], xw, AX.X, ALU.max), ("fmax", (n, j)))
                after(dve, "dve", ("fmax", (n, j)))
                done("dve", dve.tensor_tensor(feat_shift[:, n, j], half_sq[:, n, j], feat_max[:, n, j], ALU.add),
                     ("shift", (n, j)))
                after(dve, "dve", ("shift", (n, j)))
                done("dve", dve.tensor_tensor(phi[:, n, j], xw,
                                              feat_shift[:, n, j].unsqueeze(2).broadcast_to([128, H, M]),
                                              ALU.subtract), name)

            def add_eps(n, j):
                after(dve, "act", ("exp", (n, j)))
                done("dve", dve.tensor_scalar(phi[:, n, j], phi[:, n, j], SELF_EPS, None, ALU.add), ("eps", (n, j)))

            after(dve, "pe", "norm")
            done("dve", dve.tensor_copy(half_sq[:], bank("norm")[:, 0:2 * PAIRS * H].rearrange(
                "p (n j h) -> p n j h", n=2, j=PAIRS)), "norm")
            after(dve, "dve", "norm")
            for n in XW[:4]:
                features(*n)
            for n in XW[:4]:
                add_eps(*n)
            for n in XW[4:]:
                features(*n)
            for n in XW[4:]:
                add_eps(*n)
            after(dve, "pool", ("mask", HG - 1))
            for j in PR:
                after(dve, "pe", ("kv", j))
                src = bank(("kv", j))[:, 0:G * 2 * KVW].rearrange("p (n c) -> p n c", c=KVW)
                done("dve", dve.tensor_tensor(kv[:, j].rearrange("p g s c -> p (g s) c"), src,
                                              block_mask[:].unsqueeze(1).broadcast_to([128, G * 2, KVW]), ALU.mult),
                     ("kv", j))
            for j in PR:
                after(dve, "pe", ("num", j))
                num = bank(("num", j))[:, 0:G * 2 * KVW].rearrange("p (g s c) -> p g s c", g=G, s=2)
                for par in range(2):
                    rows = slice(SLOT * par, SLOT * par + SLOT)
                    done("dve", dve.tensor_scalar(den[rows, j], num[rows, :, par, HG * DK:], float(M) * SELF_EPS, None,
                                                  ALU.add), ("den" if par else "den0", j))
                after(dve, "dve", ("den", j))
                done("dve", dve.reciprocal(rden[:, j], den[:, j]), ("rden", j))
                after(dve, "dve", ("rden", j))
                for par in range(2):
                    rows = slice(SLOT * par, SLOT * par + SLOT)
                    done("dve", dve.tensor_tensor(
                        merged[rows, j].rearrange("p (g h d) -> p g h d", g=G, h=HG),
                        num[rows, :, par, 0:HG * DK].rearrange("p g (h d) -> p g h d", h=HG),
                        rden[rows, j].unsqueeze(3).broadcast_to([SLOT, G, HG, DK]), ALU.mult),
                        ("num" if par else "num0", j))
            dve.wait_ge(ffn_landed, 48)
            for i in range(3):
                done("dve", dve.tensor_scalar(ffn_nat[:, i], ffn_int[:, i], 1.0 / 127.0, None, ALU.mult), ("ffn", i))
            dve.wait_ge(bias_landed, 32)
            dve.wait_ge(x_landed, 32)
            done("dve", dve.tensor_tensor(x_sb[:], x_sb[:], sbo_sb[:].unsqueeze(1).broadcast_to([128, PAIRS, D]),
                                          ALU.add), "xbias")
            after(dve, "dve", "xbias")
            for j in PR:
                after(dve, "pe", ("self", j))
                done("dve", dve.tensor_tensor(y1[:, j], bank(("self", j))[:, 0:D], x_sb[:, j], ALU.add), ("self", j))
                after(dve, "dve", ("self", j))
                done("dve", dve.bn_stats(stats1[:, j], y1[:, j]), ("stats", j))
                after(dve, "dve", ("stats", j))
                done("dve", dve.bn_aggr(mv1[:, j], stats1[:, j]), ("aggr", j))
            after(dve, "dve", ("aggr", PAIRS - 1))
            done("dve", dve.tensor_scalar(ve1[:], mv1[:, :, 1], LN_EPS, None, ALU.add), "ve")
            after(dve, "pool", "rstd")
            for j in PR:
                done("dve", dve.tensor_scalar(x1[:, j], y1[:, j], mv1[:, j, 0:1], rstd1[:, j:j + 1], ALU.subtract,
                                              ALU.mult), ("x1", j))
            after(dve, "dve", ("x1", PAIRS - 1))
            done("dve", dve.tensor_tensor(x1b[:], x1[:], xbo_sb[:].unsqueeze(1).broadcast_to([128, PAIRS, D]),
                                          ALU.add), "x1b")
            for h in range(0, H, 2):
                after(dve, "pe", ("qk", h))
                src = bank(("qk", h))[0:C, :].rearrange("c (b s) -> c b s", b=B)[:, :, 0:S]
                done("dve", dve.tensor_copy(q_all[:].rearrange("c b (h i) -> c b h i", h=H)[:, :, h, :], src), ("qk", h))

            def context_lo(b, par, slot, unit):
                dve.wait_ge(mx_filled, slot + 1)
                dve.wait_ge(cthi_ready, TU * b + unit + 1)
                cols = slice(TW * unit, TW * unit + TW)
                dve.tensor_tensor(ct_lo[par][:, cols], mx[unit % 2][0:C, 0:TW], ct_hi[par][0:C, cols].bitcast(F32),
                                  ALU.subtract).then_inc(mx_freed, 1)

            def chunk_max(slot, at, j, c):
                dve.wait_ge(mx_filled, slot + 1)
                dve.tensor_reduce(max_part[:, j, c:c + 1], mx[at % 2][:, 0:KC], AX.X, ALU.max).then_inc(mx_freed, 1)

            def join_maxima(b, slot):
                dve.wait_ge(mx_freed, slot)
                dve.tensor_reduce(max_neg[:], max_part[:], AX.X, ALU.max, negate=True).then_inc(maxneg_ready, 1)

            def copy_maxima(b, slot, at):
                dve.wait_ge(mx_filled, slot + 1)
                dve.tensor_copy(max_row[:], mx[at % 2][0:QT, 0:128]).then_inc(mx_freed, 1)
                dve.wait_ge(mx_freed, slot + 1)
                dve.sem_inc(maxrow_ready, 1)

            def exp_lo(g, t):
                dve.wait_ge(phi_ready, g + 1)
                wait(dve, pv_done, g - 2)
                dve.tensor_tensor(p_lo[t % 3][:], p_full[t % 2][:], p_hi[t % 3][:].bitcast(F32),
                                  ALU.subtract).then_inc(plo_ready, 1)

            def reciprocals(b):
                dve.wait_ge(sums_landed, 16 * (b + 1))
                dve.reciprocal(rsums[:], sums[:]).then_inc(rsums_ready, 1)

            def step(pair, ins, name):
                ins.then_inc(out_steps, 1)
                dve.wait_ge(out_steps, out_step(pair, name))

            def layer_norm_stats(pair, src, tail):
                dve.bn_stats(stats2[:], src).then_inc(out_steps, 1)
                dve.wait_ge(out_steps, out_step(pair, "stats" + tail))
                dve.sem_inc(dve_waited, 1)
                step(pair, dve.bn_aggr(mv2[:], stats2[:]), "aggr" + tail)
                step(pair, dve.tensor_scalar(ve2[:], mv2[:, 1:2], LN_EPS, None, ALU.add), "ve" + tail)

            def output(what, pair, slot, at):
                src = mx[at % 2]
                dve.wait_ge(mx_filled, slot + 1)
                if what == "out":
                    step(pair, dve.tensor_tensor(y2[:], src[:, 0:D], x1b[:, pair, :], ALU.add), "y2")
                    dve.sem_inc(mx_freed, 1)
                    layer_norm_stats(pair, y2[:], "")
                if what == "x2T":
                    step(pair, dve.tensor_copy(x2T[:], src[:, 0:128]), "x2T")
                    dve.sem_inc(mx_freed, 1)
                if what == "gate":
                    dve.wait_ge(tanh_ready, pair + 1)
                    step(pair, dve.scalar_tensor_tensor(out=silu_g[:], in0=tanh_g[:], scalar=1.0, in1=src[:, 0:HID],
                                                        op0=ALU.add, op1=ALU.mult), "silu")
                    dve.sem_inc(mx_freed, 1)
                if what == "up":
                    step(pair, dve.scalar_tensor_tensor(out=hidT[:].rearrange("p c s -> p (c s)"), in0=silu_g[:],
                                                        scalar=0.5, in1=src[:, 0:HID], op0=ALU.mult, op1=ALU.mult), "hid")
                    dve.sem_inc(mx_freed, 1)
                if what == "down":
                    step(pair, dve.tensor_tensor(y2[:], src[:, 0:D], x2[:], ALU.add), "y3")
                    dve.sem_inc(mx_freed, 2)
                    layer_norm_stats(pair, y2[:], "3")
                    finish_norm(pair, x3[:, pair, :], 2, "x3")

            def finish_norm(pair, dst, n, name):
                dve.wait_ge(rstd_ready, 2 * pair + n)
                step(pair, dve.tensor_scalar(dst, y2[:], mv2[:, 0:1], rstd2[:], ALU.subtract, ALU.mult), name)

            def work(b, par, base, prep, pair):
                plan = ring_plan(prep, pair is not None)
                number = slots(plan)
                for t in range(KT):
                    for p in range(4):
                        if p == 2 and not (isinstance(b, int) and b == 0 and t == 0):
                            exp_lo(KT * b + t - 1, (t - 1) % KT)
                        if (t, p) not in plan:
                            continue
                        (kind, what), at = plan[(t, p)], number[(t, p)]
                        if kind == "transpose":
                            context_lo(b + 1, 1 - par, base + at, what)
                        elif kind == "max":
                            chunk_max(base + at, at, *what)
                            if what == MAXES[-1]:
                                join_maxima(b + 1, base + at + 1)
                        elif kind == "maxrow":
                            copy_maxima(b + 1, base + at, at)
                        else:
                            output(kind, pair, base + at, at)
                    if t == 3 and not (isinstance(b, int) and b == 0):
                        reciprocals(b - 1)
                    if t == 7 and pair is not None:
                        finish_norm(pair, x2[:], 1, "x2")

            for unit in range(TU):
                context_lo(0, 0, unit, unit)
            for n, (j, c) in enumerate(MAXES):
                chunk_max(TU + n, TU + n, j, c)
            join_maxima(0, PREP_SLOTS - 1)
            copy_maxima(0, PREP_SLOTS - 1, PREP_SLOTS - 1)
            sequence_loop(dve, work)
            exp_lo(KT * B - 1, KT - 1)
            reciprocals(B - 1)
            for n, what in enumerate(FINAL):
                output(what, PAIRS - 1, LAST_BASE + n, n)
                if what == "out":
                    finish_norm(PAIRS - 1, x2[:], 1, "x2")

        @block.tensor
        def _(pe):
            def fill(name):
                n = FILL_AT[name]
                if n >= 8:
                    before, engine = FILLS[n - 8]
                    after(pe, engine, before)
                return banks[n % 8]

            def mm(dst, lhsT, rhs, start=True, stop=True):
                return pe.matmul(dst, lhsT, rhs, start=start, stop=stop, skip_group_check=True)

            after(pe, "pool", "ident")
            pe.wait_ge(x_landed, 32)
            dst = fill("xT")
            for j in PR:
                last = pe.transpose(dst[:, 128 * j:128 * j + 128], x_sb[:, j], ident[:])
            done("pe", last, "xT")
            pe.wait_ge(self_landed, 64)
            dst = fill("wT")
            for n in range(4):
                last = pe.transpose(dst[:, 128 * n:128 * n + 128], w_self[:, n], ident[:])
            done("pe", last, "wT")
            after(pe, "pool", ("wide", HG - 1))
            dst = fill("projT")
            for g in range(G):
                last = pe.transpose(dst[:, 128 * g:128 * g + 128], proj_wide[:, g].rearrange("p h d -> p (h d)"), ident[:])
            done("pe", last, "projT")
            after(pe, "act", "xT")
            after(pe, "dve", "wT")
            done("pe", mm(fill("kT"), wT_self[:, 1], xT[:]), "kT")
            done("pe", mm(fill("qT"), wT_self[:, 0], xT[:]), "qT")
            dst = fill("v")
            for j in PR:
                last = mm(dst[:, 128 * j:128 * j + 128], xT[:, 128 * j:128 * j + 128], wT_self[:, 2])
            done("pe", last, "v")
            after(pe, "pool", "norm2")
            dst = fill("norm")
            for n, j in XW:
                after(pe, "act", f"square{n}")
                at = (n * PAIRS + j) * H
                last = mm(dst[:, at:at + H], kq_sq[:, n, 128 * j:128 * j + 128], half_norm[:])
            done("pe", last, "norm")

            def random_features(n, j):
                after(pe, "act", "projT")
                after(pe, "dve", "qT" if n else "kT")
                done("pe", mm(fill(("xw", (n, j))), kq_scaled[:, n, 128 * j:128 * j + 128], projT[:]), ("xw", (n, j)))

            def weight_transposes(w, i):
                src = {"q": wq_nat, "k": wk_nat, "v": wv_nat}[w]
                width = D if w == "q" else C
                dst = fill(("wT", (w, i)))
                for n in range(4):
                    cols = slice(128 * (4 * i + n), 128 * (4 * i + n) + 128)
                    last = pe.transpose(dst[:, width * n:width * n + width], src[:, cols], ident[0:width, 0:width])
                done("pe", last, ("wT", (w, i)))

            def head_products(name, i, par, lhs, rhs, lhs_width, width):
                dst = fill((name, (i, par)))
                rows = slice(XD * par, XD * par + XD)
                for n in range(4):
                    last = mm(dst[0:lhs_width, width * n:width * n + width], lhs[rows, 4 * i + n, :],
                              rhs[rows, 4 * i + n, :])
                done("pe", last, (name, (i, par)))

            for n in XW[:4]:
                random_features(*n)
            pe.wait_ge(xw_landed, 64)
            for n in WT:
                weight_transposes(*n)
            for n in XW[4:]:
                random_features(*n)
            after(pe, "act", ("wT", WT[-1]))
            for i, par in AB:
                head_products("wqk", i, par, wqT, wkT, D, C)
            after(pe, "act", "v")
            for j in PR:
                after(pe, "dve", ("eps", (0, j)))
                dst = fill(("kv", j))
                for g in range(G):
                    last = mm(dst[:, 2 * KVW * g:2 * KVW * (g + 1)].rearrange("p (s c) -> p s c", s=2),
                              phi[:, 0, j, HG * g:HG * g + HG, :].rearrange("p h m -> p (h m)"), v_masked[:, j, :, g, :])
                done("pe", last, ("kv", j))
            for j in PR:
                after(pe, "dve", ("eps", (1, j)))
                dst = fill(("phiqT", j))
                for g in range(G):
                    last = pe.transpose(dst[:, 128 * g:128 * g + 128],
                                        phi[:, 1, j, HG * g:HG * g + HG, :].rearrange("p h m -> p (h m)"), ident[:])
                done("pe", last, ("phiqT", j))
            for j in PR:
                after(pe, "act", ("phiqT", j))
                after(pe, "dve", ("kv", j))
                dst = fill(("num", j))
                for g in range(G):
                    last = mm(dst[:, 2 * KVW * g:2 * KVW * (g + 1)], phiqT[:, j, g, :],
                              kv[:, j, g].rearrange("p s c -> p (s c)"))
                done("pe", last, ("num", j))
            for n in WV:
                weight_transposes(*n)
            for i in range(3):
                after(pe, "dve", ("ffn", i))
                dst = fill(("ffnT", i))
                for c in range(HC):
                    last = pe.transpose(dst[:, 128 * c:128 * c + 128], ffn_nat[:, i, c], ident[:])
                done("pe", last, ("ffnT", i))
            after(pe, "act", ("wT", WV[-1]))
            for i, par in AB:
                head_products("wvo", i, par, wvT, wo_nat, C, D)
            for j in PR:
                after(pe, "dve", ("num", j))
                done("pe", pe.transpose(fill(("mergedT", j))[:, 0:128], merged[:, j], ident[:]), ("mergedT", j))
            for j in PR:
                after(pe, "act", ("mergedT", j))
                done("pe", mm(fill(("self", j))[:, 0:D], mergedT[:, j], wT_self[:, 3]), ("self", j))
            for j in PR:
                after(pe, "dve", ("x1", j))
                done("pe", pe.transpose(fill(("x1T", j))[:, 0:128], x1[:, j], ident[:]), ("x1T", j))
            after(pe, "act", ("x1T", PAIRS - 1))
            for h in range(H):
                done("pe", mm(fill(("qk", h))[0:C, :], wqk[:, h], x1T[:]), ("qk", h))

            def ring(slot):
                wait(pe, mx_freed, slot - 1)

            def context_transposes(b, par, slot, unit, landed):
                ring(slot)
                pe.wait_ge(ctx_landed[par], 16 * landed)
                for n in range(KT // TU):
                    last = pe.transpose(mx[unit % 2][0:C, KP * n:KP * n + KP], ctx_nat[:, par, 3 * unit + n],
                                        ident[0:KP, 0:KP])
                last.then_inc(mx_filled, 1)

            def max_scores(b, par, slot, at, j, c):
                ring(slot)
                pe.wait_ge(qhi_ready, b + 1)
                pe.wait_ge(cthi_ready, TU * (b + 1))
                mm(mx[at % 2][:, 0:KC], q_hi[par][0:C, 128 * j:128 * j + 128],
                   ct_hi[par][0:C, KC * c:KC * c + KC]).then_inc(mx_filled, 1)

            def turn_maxima(b, slot, at):
                ring(slot)
                pe.wait_ge(maxneg_ready, b + 1)
                pe.transpose(mx[at % 2][0:QT, 0:128], max_neg[:], ident[:]).then_inc(mx_filled, 1)

            def scores(g, t, par, half):
                dst = sc[t % 2][0:KP, half, 0:QH]
                cols, keys = slice(QH * half, QH * half + QH), slice(t, NCTX, KT)
                keys = slice(KP * t, KP * t + KP)
                mm(dst, ct_hi[par][:, keys], q_hi[par][:, cols], True, False)
                mm(dst, ct_lo[par][:, keys], q_hi[par][0:C, cols], False, False)
                last = mm(dst, ct_hi[par][0:C, keys], q_lo[par][:, cols], False, True)
                if half:
                    last.then_inc(scores_ready, 1)

            def context_sum(t, par, half):
                dst = acc[0:C + 1, half, 0:QH]
                cols = slice(QH * half, QH * half + QH)
                mm(dst, cn_hi[par][:, t], p_hi[t % 3][:, cols], t == 0, False)
                mm(dst, cn_lo[par][:, t], p_hi[t % 3][:, cols], False, False)
                last = mm(dst, cn_hi[par][:, t], p_lo[t % 3][:, cols], False, t == KT - 1)
                if half:
                    last.then_inc(pv_done, 1)

            def output(what, pair, slot, at):
                ring(slot)
                dst = mx[at % 2]
                if what == "out":
                    pe.wait_ge(unorm_ready, 2 * pair + 2)
                    for h in range(H):
                        last = mm(dst[:, 0:D], u_norm[:, h].rearrange("c p s -> c (p s)"), wvo[:, h], h == 0, h == H - 1)
                if what == "x2T":
                    pe.wait_ge(out_steps, out_step(pair, "x2"))
                    last = pe.transpose(dst[:, 0:128], x2[:], ident[:])
                if what in ("gate", "up"):
                    pe.wait_ge(out_steps, out_step(pair, "x2T"))
                    for c in range(HC):
                        last = mm(dst[:, 128 * c:128 * c + 128], ffnT[:, 0 if what == "gate" else 1, c], x2T[:])
                if what == "down":
                    pe.wait_ge(out_steps, out_step(pair, "hid"))
                    for c in range(HC):
                        last = mm(dst[:, 0:D], hidT[:, c], ffnT[:, 2, c], c == 0, c == HC - 1)
                last.then_inc(mx_filled, 2 if what == "down" else 1)

            def sum_step(b, t, par, part):
                if part == 0:
                    pe.wait_ge(plo_ready, KT * b + t + 1)
                    if t == 0:
                        wait(pe, u_ready, b)
                        pe.wait_ge(nat_ready, b + 1)
                context_sum(t, par, part)

            def work(b, par, base, prep, pair, landed):
                plan = ring_plan(prep, pair is not None)
                number = slots(plan)

                def extra(t, p):
                    if (t, p) not in plan:
                        return
                    (kind, what), at = plan[(t, p)], number[(t, p)]
                    if kind == "transpose":
                        context_transposes(b + 1, 1 - par, base + at, what, landed)
                    elif kind == "max":
                        max_scores(b + 1, 1 - par, base + at, at, *what)
                    elif kind == "maxrow":
                        turn_maxima(b + 1, base + at, at)
                    else:
                        output(kind, pair, base + at, at)

                first = isinstance(b, int) and b == 0
                for t in range(KT):
                    extra(t, 0)
                    g = KT * b + t
                    if t == 0:
                        pe.wait_ge(maxrow_landed, 16 * (b + 1))
                        pe.wait_ge(qlo_ready, b + 1)
                    wait(pe, phi_ready, g - 1)
                    scores(g, t, par, 0)
                    extra(t, 1)
                    scores(g, t, par, 1)
                    extra(t, 2)
                    if t >= 2:
                        sum_step(b, t - 2, par, 0)
                    elif not first:
                        sum_step(b - 1, KT + t - 2, 1 - par, 0)
                    extra(t, 3)
                    if t >= 2:
                        sum_step(b, t - 2, par, 1)
                    elif not first:
                        sum_step(b - 1, KT + t - 2, 1 - par, 1)

            after(pe, "dve", ("qk", H - 2))
            after(pe, "act", ("qk", H - 1))
            after(pe, "pool", "ones0")
            for unit in range(TU):
                context_transposes(0, 0, unit, unit, 1)
            for n, (j, c) in enumerate(MAXES):
                max_scores(0, 0, TU + n, TU + n, j, c)
            turn_maxima(0, PREP_SLOTS - 1, PREP_SLOTS - 1)

            per = 2 * PREP_SLOTS + OUT_SLOTS
            work(0, 0, PREP_SLOTS, True, None, 1)
            with pe.Fori(0, 3) as k:
                work(2 * k + 1, 1, per * k + 2 * PREP_SLOTS, True, None, k + 2)
                work(2 * k + 2, 0, per * k + 3 * PREP_SLOTS, True, k, k + 2)
            work(B - 1, 1, LAST_BASE, False, None, None)
            for t in (KT - 2, KT - 1):
                for half in range(2):
                    sum_step(B - 1, t, 1, half)
            for n, what in enumerate(FINAL):
                output(what, PAIRS - 1, LAST_BASE + n, n)


_INS = ['x', 'ctx_768', 'L0_attn_Wq', 'L0_attn_Wk', 'L0_attn_Wv', 'L0_attn_Wo', 'L0_attn_bo', 'L0_attn_proj',
        'L0_xattn_Wq', 'L0_xattn_Wk', 'L0_xattn_Wv', 'L0_xattn_Wo', 'L0_xattn_bo',
        'L0_ffn_w_gate', 'L0_ffn_w_up', 'L0_ffn_w_down']
_OUTS = [((B, S, D), 'float32')]


def kernel(**inputs):
    import numpy as _np
    import concourse.bacc as _bacc
    from concourse import mybir as _mybir
    from concourse.bass_utils import run_bass_kernel_spmd as _run

    nc = _bacc.Bacc("TRN2", target_bir_lowering=False, num_devices=1)
    arrays, args = {}, []
    for name in _INS:
        a = _np.ascontiguousarray(inputs[name])
        arrays[f"in_{name}_dram"] = a
        args.append(nc.dram_tensor(f"in_{name}_dram", a.shape, _mybir.dt.from_np(a.dtype), kind="ExternalInput").ap())
    for i, (shape, dtype) in enumerate(_OUTS):
        dt = _mybir.dt.from_np(_np.dtype(dtype))
        args.append(nc.dram_tensor(f"out_{i}_dram", shape, dt, kind="ExternalOutput").ap())
    program(nc, *args)
    r = _run(nc, [arrays], core_ids=[0])
    got = tuple(r.results[0][f"out_{i}_dram"] for i in range(len(_OUTS)))
    return got[0]
```

```python
from contextlib import ExitStack

import concourse.bass as bass
from concourse import mybir

F32 = mybir.dt.float32
F32R = mybir.dt.float32r
I32 = mybir.dt.int32
ALU = mybir.AluOpType
ACT = mybir.ActivationFunctionType
AX = mybir.AxisListType

B, S, D = 8, 56, 128
SLOT = 64
PAIRS = B // 2
H = 16
DK = D // H
M = 32
G = 4
HG = H // G
KVW = HG * DK + HG
SELF_EPS = 1e-6
C, NCTX = 96, 1500
KT, KP = 12, 125
XD = 64
Q = H * S
QH = Q // 2
QT = Q // 128
KC = NCTX // 3
TU = 4
TW = NCTX // TU
HID = 384
HC = HID // 128
LN_EPS = 1e-5
SUM_P = 112

MAXES = [(j, c) for c in range(3) for j in range(QT)]


def ring_plan(prep, output):
    plan = {}
    if prep:
        for u, at in enumerate([(0, 0), (0, 2), (1, 0), (1, 2)]):
            plan[at] = ("transpose", u)
        places = sorted([(t, p) for t in range(2, 10) for p in (1, 3)] + [(t, 2) for t in range(2, 7)])
        for at, what in zip(places, MAXES):
            plan[at] = ("max", what)
        plan[(10, 3)] = ("maxrow", None)
    if output:
        plan[(7, 2)] = ("out", None)
        plan[(9, 2)] = ("x2T", None)
        plan[(10, 0)] = ("gate", None)
        plan[(10, 1)] = ("up", None)
        plan[(11, 2)] = ("down", None)
    return plan


PREP_SLOTS = 26
OUT_SLOTS = 6


def program(nc, x, ctx_in, sWq, sWk, sWv, sWo, sbo, proj, xWq, xWk, xWv, xWo, xbo, w_gate, w_up, w_down, out):
    with ExitStack() as stack:
        def sb(name, shape, dt=F32):
            return stack.enter_context(nc.sbuf_tensor(name, shape, dt))

        def ps(name, shape):
            return stack.enter_context(nc.psum_tensor(name, shape, F32))

        def sem(name):
            return stack.enter_context(nc.semaphore(name))

        ident = sb("ident", [128, 128])
        block_mask = sb("block_mask", [128, KVW])
        half_norm = sb("half_norm", [128, H])
        minus_half = sb("minus_half", [128, PAIRS])
        wT_self = sb("wT_self", [128, 4, 128])
        proj_sb = sb("proj_sb", [128, G, DK])
        sbo_sb = sb("sbo_sb", [128, D])
        xbo_sb = sb("xbo_sb", [128, D])
        wqk = sb("wqk", [128, H, C])
        wvo = sb("wvo", [C, H, D])
        ffn_int = sb("ffn_int", [128, 3, HC, 128], I32)
        ffn_nat = sb("ffn_nat", [128, 3, HC, 128])
        ffnT = sb("ffnT", [128, 3, HC, 128])

        x_sb = sb("x_sb", [128, PAIRS, D])
        half_sq = sb("half_sq", [128, 2, PAIRS, H])
        feat_max = sb("feat_max", [128, 2, PAIRS, H])
        feat_shift = sb("feat_shift", [128, 2, PAIRS, H])
        den = sb("den", [128, PAIRS, G, HG])
        rden = sb("rden", [128, PAIRS, G, HG])
        merged = sb("merged", [128, PAIRS, D])
        mergedT = sb("mergedT", [128, PAIRS, D])
        y1 = sb("y1", [128, PAIRS, D])
        stats1 = sb("stats1", [128, PAIRS, 6])
        mv1 = sb("mv1", [128, PAIRS, 2])
        ve1 = sb("ve1", [128, PAIRS])
        rstd1 = sb("rstd1", [128, PAIRS])
        x1 = sb("x1", [128, PAIRS, D])
        x1b = sb("x1b", [128, PAIRS, D])
        x1T = sb("x1T", [128, 512])

        q_all = sb("q_all", [C, B, Q])
        ctx_nat = sb("ctx_nat", [KP, 2, KT, C])
        cn_hi = [sb("cn_hi0", [KP, KT, C + 1], F32R)]
        cn_lo = [sb("cn_lo0", [KP, KT, C + 1], F32R)]
        ct_hi = [sb("ct_hi0", [C + 1, NCTX], F32R)]
        ct_lo = [sb("ct_lo0", [C, NCTX], F32R)]
        q_hi = [sb("q_hi0", [C + 1, Q], F32R)]
        q_lo = [sb("q_lo0", [C, Q], F32R)]
        max_part = sb("max_part", [128, QT, 3])
        max_neg = sb("max_neg", [128, QT])
        max_row = sb("max_row", [QT, 128], F32R)
        sums = sb("sums", [SUM_P, Q // SUM_P])
        rsums = sb("rsums", [SUM_P, Q // SUM_P])
        u_norm = sb("u_norm", [C, H, 2, SLOT])

        stats2 = sb("stats2", [128, 6])
        mv2 = sb("mv2", [128, 2])
        ve2 = sb("ve2", [128, 1])
        rstd2 = sb("rstd2", [128, 1])
        x3 = sb("x3", [128, PAIRS, D])

        setup_only = ExitStack()

        def early(name, shape, dt=F32):
            return setup_only.enter_context(nc.sbuf_tensor(name, shape, dt))

        w_self = early("w_self", [128, 4, 128])
        proj_wide = early("proj_wide", [128, G, H, DK])
        projT = early("projT", [128, 512])
        kq_scaled = early("kq_scaled", [128, 2, 512])
        kq_sq = early("kq_sq", [128, 2, 512])
        v_masked = early("v_masked", [128, PAIRS, 2, G, KVW])
        phi = early("phi", [128, 2, PAIRS, H, M])
        kv = early("kv", [128, PAIRS, G, 2, KVW])
        phiqT = early("phiqT", [128, PAIRS, G, 128])
        wq_nat = early("wq_nat", [128, H * XD])
        wk_nat = early("wk_nat", [C, H * XD])
        wv_nat = early("wv_nat", [C, H * XD])
        wo_nat = early("wo_nat", [128, 8, D])
        wqT = early("wqT", [128, 8, D])
        wkT = early("wkT", [128, 8, C])
        wvT = early("wvT", [128, 8, C])
        xT = early("xT", [128, 512])
        setup_only.close()
        for pair_of, name, shape in (
                (cn_hi, "cn_hi1", [KP, KT, C + 1]), (cn_lo, "cn_lo1", [KP, KT, C + 1]), (ct_hi, "ct_hi1", [C + 1, NCTX]),
                (ct_lo, "ct_lo1", [C, NCTX]), (q_hi, "q_hi1", [C + 1, Q]), (q_lo, "q_lo1", [C, Q])):
            pair_of.append(sb(name, shape, F32R))
        p_full = [sb(f"p_full{i}", [KP, Q]) for i in range(2)]
        p_hi = [sb(f"p_hi{i}", [KP, Q], F32R) for i in range(3)]
        p_lo = [sb(f"p_lo{i}", [KP, Q], F32R) for i in range(3)]
        u = sb("u", [C + 1, Q])
        rsum_row = sb("rsum_row", [1, Q])
        rsum_all = sb("rsum_all", [C, Q])
        y2 = sb("y2", [128, D])
        x2 = sb("x2", [128, D])
        x2T = sb("x2T", [128, 128])
        tanh_g = sb("tanh_g", [128, HID])
        silu_g = sb("silu_g", [128, HID])
        hidT = sb("hidT", [128, HC, 128])

        sc = [ps(f"sc{i}", [128, 2, 512]) for i in range(2)]
        acc = ps("acc", [128, 2, 512])
        mx = [ps(f"mx{i}", [128, 512]) for i in range(2)]
        banks = [sc[0][:, 0, :], sc[0][:, 1, :], sc[1][:, 0, :], sc[1][:, 1, :],
                 acc[:, 0, :], acc[:, 1, :]]

        PR = range(PAIRS)
        XW = [(n, j) for n in (0, 1) for j in PR]
        AB = [(i, par) for i in range(2) for par in range(2)]
        def xw(n, j):
            return ("xw", (n, j)), "dve"

        def wt(w, i):
            return ("wT", (w, i)), "act"

        def of_heads(name, i, par):
            return (name, (i, par)), "act"

        def act_(name, i):
            return (name, i), "act"

        def dve_(name, i):
            return (name, i), "dve"

        FILLS = ([("xT", "dve"), ("wT_kq", "dve"), ("kT", "dve"), ("projT", "act"), ("qT", "dve"), xw(0, 0),
                  dve_("norm", 0), xw(0, 1), ("wT_vo", "act"), dve_("norm", 1), ("v", "act"), xw(0, 2), wt("q", 0),
                  xw(0, 3), wt("k", 0), xw(1, 0), of_heads("wqk", 0, 0), xw(1, 1), of_heads("wqk", 0, 1), wt("q", 1),
                  xw(1, 2), wt("k", 1), wt("v", 0), xw(1, 3), wt("v", 1), of_heads("wqk", 1, 0),
                  dve_("kv", 0), of_heads("wqk", 1, 1), dve_("kv", 1), dve_("kv", 2), dve_("kv", 3),
                  act_("phiqT", 0), act_("phiqT", 1), dve_("num", 0), act_("phiqT", 2), dve_("num", 1),
                  act_("phiqT", 3), dve_("num", 2), act_("mergedT", 0), dve_("num", 3), dve_("self", 0),
                  act_("mergedT", 1), of_heads("wvo", 0, 0), dve_("self", 1), act_("mergedT", 2),
                  of_heads("wvo", 0, 1), dve_("self", 2), dve_("x1T", 0), act_("q0", 0), act_("q0", 1), act_("mergedT", 3),
                  of_heads("wvo", 1, 0), dve_("self", 3), of_heads("wvo", 1, 1)]
                 + [act_("ffnT", i) for i in range(3)] + [act_("x1T", j) for j in PR[1:]]
                 + [act_("qk", h) for h in range(H)])
        FILL_AT = {name: i for i, (name, _) in enumerate(FILLS)}

        ACT_SETUP = (["projT", "square0", "square1", ("exp", (0, 0)), "wT_vo", "v0", "v", ("exp", (0, 1)),
                      ("wT", ("q", 0)), ("exp", (0, 2)), ("wT", ("k", 0)), ("exp", (0, 3)), ("wqk", (0, 0)),
                      ("exp", (1, 0)), ("wqk", (0, 1)), ("wT", ("q", 1)), ("exp", (1, 1)), ("wT", ("k", 1)),
                      ("wT", ("v", 0)), ("exp", (1, 2)), ("wT", ("v", 1)), ("wqk", (1, 0)), ("exp", (1, 3)),
                      ("wqk", (1, 1))]
                     + [("phiqT", j) for j in PR]
                     + [("mergedT", 0), ("mergedT", 1), ("wvo", (0, 0)), ("mergedT", 2), ("wvo", (0, 1)),
                        "q0_hi0", ("q0", 0), ("mergedT", 3), ("q0", 1), ("wvo", (1, 0)), ("wvo", (1, 1))]
                     + [("ffnT", i) for i in range(3)] + [("x1T", j) for j in PR[1:]]
                     + [("qk", h) for h in range(H)])

        def numerator_steps(j):
            return [("den0", j), ("den", j), ("rden", j), ("num0", j), ("num", j)]

        def residual_steps(j):
            return [("self", j), ("stats", j), ("aggr", j)]

        DVE_SETUP = (["xT", "wT_kq", "kT", "qT"]
                     + [s for i in range(2) for s in (("fmax", XW[i]), ("norm", i), ("shift", XW[i]), ("xw", XW[i]))]
                     + ["xbias"]
                     + [s for n in XW[2:4] for s in (("fmax", n), ("shift", n), ("xw", n))]
                     + [s for i in range(4) for s in (("eps", XW[i]), ("fmax", XW[4 + i]), ("shift", XW[4 + i]),
                                                      ("xw", XW[4 + i]))]
                     + [s for j in PR for s in (("kv", j), ("eps", (1, j)))]
                     + numerator_steps(0) + numerator_steps(1) + numerator_steps(2)
                     + residual_steps(0) + ["ve0"] + numerator_steps(3) + residual_steps(1)
                     + [("x1", 0)] + residual_steps(2) + [("x1T", 0)] + [("ffn", i) for i in range(3)]
                     + ["q0_hi1"] + residual_steps(3)
                     + ["ve"] + [("x1", j) for j in PR[1:]] + ["x1b"])
        POOL_SETUP = (["x_zero", "ident0", "ident", "wide_zero", "norm0", "norm1", "norm2", "mask0", "v_zero",
                       "minus_half"] + [("wide", hl) for hl in range(HG)] + [("mask", hl) for hl in range(HG)]
                      + [("ones", 0), ("ones", 1), "unorm_zero", "ones_nat0", "ones0", "rstd0", "rstd", "ones_nat1", "ones1"])
        setup = {"act": sem("act_setup"), "dve": sem("dve_setup"), "pool": sem("pool_setup"), "pe": sem("pe_setup")}
        ORDER = {"act": ACT_SETUP, "dve": DVE_SETUP, "pool": POOL_SETUP, "pe": [n for n, _ in FILLS]}
        COUNT = {e: {n: i + 1 for i, n in enumerate(names)} for e, names in ORDER.items()}
        said = {e: 0 for e in ORDER}

        def done(engine, ins, name):
            assert ORDER[engine][said[engine]] == name, (engine, name, ORDER[engine][said[engine]])
            said[engine] += 1
            ins.then_inc(setup[engine], 1)

        def after(eng, engine, name):
            eng.wait_ge(setup[engine], COUNT[engine][name])

        x_landed = sem("x_landed")
        wkq_landed = sem("wkq_landed")
        wvo_landed = sem("wvo_landed")
        xqk_landed = sem("xqk_landed")
        proj_landed = sem("proj_landed")
        bias_landed = sem("bias_landed")
        xvo_landed = sem("xvo_landed")
        ffn_landed = sem("ffn_landed")
        ctx_landed = [sem(f"ctx_landed{i}") for i in range(2)]
        scores_ready = sem("scores_ready")
        phi_ready = sem("phi_ready")
        plo_ready = sem("plo_ready")
        p_ready = sem("p_ready")
        pv_done = sem("pv_done")
        u_ready = sem("u_ready")
        mx_filled = sem("mx_filled")
        mx_freed = sem("mx_freed")
        cthi_ready = sem("cthi_ready")
        qhi_ready = sem("qhi_ready")
        qlo_ready = sem("qlo_ready")
        nathi_ready = sem("nathi_ready")
        nat_ready = sem("nat_ready")
        maxneg_ready = sem("maxneg_ready")
        maxrow_ready = sem("maxrow_ready")
        maxrow_landed = sem("maxrow_landed")
        sums_landed = sem("sums_landed")
        rsums_ready = sem("rsums_ready")
        rrow_landed = sem("rrow_landed")
        rall_ready = sem("rall_ready")
        unorm_ready = sem("unorm_ready")
        out_steps = sem("out_steps")
        rstd_ready = sem("rstd_ready")
        tanh_ready = sem("tanh_ready")
        stored = sem("stored")

        OUT_STEPS = ["y2", "stats", "aggr", "ve", "x2", "x2T", "silu", "hid", "y3", "stats3", "aggr3", "ve3", "x3"]

        def out_step(pair, name):
            return len(OUT_STEPS) * pair + OUT_STEPS.index(name) + 1

        def ring_base(b, par):
            pairs_out = 0 if isinstance(b, int) and b == 0 else None
            if pairs_out is None:
                if isinstance(b, int):
                    pairs_out = (b - 1) // 2
                    return PREP_SLOTS * (b + 1) + OUT_SLOTS * pairs_out
                k = b[1]
                return PREP_SLOTS * (2 * k + (1 if par else 2)) + PREP_SLOTS + OUT_SLOTS * k
            return PREP_SLOTS

        block = stack.enter_context(nc.Block())

        def slots(plan):
            n, number = 0, {}
            for at in sorted(plan):
                number[at] = n
                n += 2 if plan[at][0] == "down" else 1
            return number

        def sequence_loop(eng, work):
            work(0, 0, PREP_SLOTS, True, None, 1)
            with eng.Fori(0, 3) as k:
                per = 2 * PREP_SLOTS + OUT_SLOTS
                work(2 * k + 1, 1, per * k + 2 * PREP_SLOTS, True, None, k + 2)
                work(2 * k + 2, 0, per * k + 3 * PREP_SLOTS, True, k, k + 2)
            work(B - 1, 1, 3 * (2 * PREP_SLOTS + OUT_SLOTS) + 2 * PREP_SLOTS, False, None, None)

        LAST_BASE = 3 * (2 * PREP_SLOTS + OUT_SLOTS) + 2 * PREP_SLOTS
        FINAL = ["out", "x2T", "gate", "up", "down"]

        def wait(eng, s, value):
            if isinstance(value, int) and value <= 0:
                return
            eng.wait_ge(s, value)

        pool_waited = sem("pool_waited")
        dve_waited = sem("dve_waited")

        @block.sync
        def _(sp):
            after(sp, "pool", "x_zero")
            for par in range(2):
                sp.dma_start(x_sb[SLOT * par:SLOT * par + S, :, :],
                             x.rearrange("(j p) i d -> p i j d", p=2)[par]).then_inc(x_landed, 16)
            sp.dma_start(w_self[:, 2, :], sWv).then_inc(wvo_landed, 16)
            sp.dma_start(w_self[:, 3, :], sWo).then_inc(wvo_landed, 16)
            sp.dma_start(wv_nat[:], xWv).then_inc(xvo_landed, 16)
            sp.dma_start(wo_nat[:], xWo.rearrange("(n p) d -> p n d", p=128)).then_inc(xvo_landed, 16)
            for dst, bias in ((sbo_sb, sbo), (xbo_sb, xbo)):
                sp.dma_start(dst[:], bias.rearrange("(a d) -> a d", a=1).broadcast_to([128, D])).then_inc(bias_landed, 16)
            for b in range(2):
                sp.dma_start(ctx_nat[:, b], ctx_in[b].rearrange("(p t) c -> p t c", t=KT)).then_inc(ctx_landed[b], 16)
            sp.dma_start(ffn_int[:, 0], w_gate.rearrange("(c p) d -> p c d", p=128)).then_inc(ffn_landed, 16)
            sp.dma_start(ffn_int[:, 1], w_up.rearrange("(c p) d -> p c d", p=128)).then_inc(ffn_landed, 16)
            sp.dma_start(ffn_int[:, 2], w_down.rearrange("p (c h) -> p c h", c=HC)).then_inc(ffn_landed, 16)

            def place_maxima(par):
                sp.dma_start(q_hi[par][C:C + 1, :].rearrange("a (j q) -> a j q", j=QT).bitcast(F32),
                             max_row[:, :].bitcast(F32)).then_inc(maxrow_landed, 16)

            def work(b, par, load):
                if load:
                    wait(sp, cthi_ready, TU * (b + 1))
                    wait(sp, nat_ready, b + 1)
                    src = ctx_in[b + 2].rearrange("(p t) c -> p t c", t=KT)
                    sp.dma_start(ctx_nat[:, par], src).then_inc(ctx_landed[par], 16)
                if not (isinstance(b, int) and b == B - 1):
                    sp.wait_ge(maxrow_ready, b + 2)
                    place_maxima(1 - par)
                sp.wait_ge(u_ready, 2 * b + 2)
                sp.dma_start(sums[:], u[C:C + 1, :].rearrange("a (p n) -> a p n", p=SUM_P)).then_inc(sums_landed, 16)
                sp.wait_ge(rsums_ready, b + 1)
                sp.dma_start(rsum_row[0:1, :].rearrange("a (p n) -> a p n", p=SUM_P), rsums[:]).then_inc(rrow_landed, 16)

            sp.wait_ge(maxrow_ready, 1)
            place_maxima(0)
            with sp.Fori(0, 3) as k:
                work(2 * k, 0, True)
                work(2 * k + 1, 1, True)
            work(B - 2, 0, False)
            work(B - 1, 1, False)
            sp.wait_ge(out_steps, out_step(PAIRS - 1, "x3"))
            for par in range(2):
                sp.dma_start(out.rearrange("(j p) i d -> p i j d", p=2)[par],
                             x3[SLOT * par:SLOT * par + S, :, :]).then_inc(stored, 16)
            sp.wait_ge(stored, 32)

        @block.gpsimd
        def _(pool):
            done("pool", pool.memset(x_sb[:], 0.0), "x_zero")
            done("pool", pool.memset(ident[:], 0.0), "ident0")
            after(pool, "pool", "ident0")
            done("pool", pool.affine_select(out=ident[:], in_=ident[:], compare_op=ALU.not_equal, fill=1.0, base=0,
                                            pattern=[[-1, 128]], channel_multiplier=1), "ident")
            done("pool", pool.memset(proj_wide[:], 0.0), "wide_zero")
            done("pool", pool.memset(half_norm[:], 0.5), "norm0")
            after(pool, "pool", "norm0")
            done("pool", pool.affine_select(out=half_norm[:], in_=half_norm[:], compare_op=ALU.is_ge, fill=0.0, base=0,
                                            pattern=[[-DK, H]], channel_multiplier=1), "norm1")
            after(pool, "pool", "norm1")
            done("pool", pool.affine_select(out=half_norm[:], in_=half_norm[:], compare_op=ALU.is_ge, fill=0.0, base=DK - 1,
                                            pattern=[[DK, H]], channel_multiplier=-1), "norm2")
            done("pool", pool.memset(block_mask[:], 0.0), "mask0")
            done("pool", pool.memset(v_masked[:], 0.0), "v_zero")
            done("pool", pool.memset(minus_half[:], -0.5), "minus_half")
            pool.wait_ge(proj_landed, 16)
            for hl in range(HG):
                rows = slice(M * hl, M * hl + M)
                after(pool, "pool", ("wide", hl - 1) if hl else "minus_half")
                for g in range(G):
                    last = pool.tensor_copy(proj_wide[rows, g, HG * g + hl, :], proj_sb[rows, g, :])
                done("pool", last, ("wide", hl))
            for hl in range(HG):
                rows = slice(M * hl, M * hl + M)
                after(pool, "pool", ("mask", hl - 1) if hl else ("wide", HG - 1))
                pool.memset(block_mask[rows, DK * hl:DK * hl + DK], 1.0)
                done("pool", pool.memset(block_mask[rows, HG * DK + hl:HG * DK + hl + 1], 1.0), ("mask", hl))
            for par in range(2):
                after(pool, "pool", ("ones", par - 1) if par else ("mask", HG - 1))
                for j in PR:
                    last = pool.memset(v_masked[SLOT * par:SLOT * par + S, j, par, :, HG * DK:], 1.0)
                done("pool", last, ("ones", par))
            after(pool, "pool", ("ones", 1))
            done("pool", pool.memset(u_norm[:], 0.0), "unorm_zero")
            pool.memset(cn_hi[0][:, :, C:C + 1].bitcast(F32), 1.0)
            done("pool", pool.memset(cn_lo[0][:, :, C:C + 1].bitcast(F32), 0.0), "ones_nat0")
            after(pool, "pool", "ones_nat0")
            done("pool", pool.memset(ct_hi[0][C:C + 1, :].bitcast(F32), 1.0), "ones0")
            after(pool, "pool", "ones0")
            def split_queries(b, par):
                pool.wait_ge(qhi_ready, b + 1)
                if isinstance(b, int) and b == 0:
                    after(pool, "act", ("q0", 1))
                pool.sem_inc(pool_waited, 1)
                pool.tensor_tensor(q_lo[par][:], q_all[:, b, :], q_hi[par][0:C, :].bitcast(F32),
                                   ALU.subtract).then_inc(qlo_ready, 1)

            def split_context(b, par):
                pool.wait_ge(ctx_landed[par], 16 * landing(b, par))
                pool.wait_ge(nathi_ready, b + 1)
                pool.sem_inc(pool_waited, 1)
                pool.tensor_tensor(cn_lo[par][:, :, 0:C], ctx_nat[:, par], cn_hi[par][:, :, 0:C].bitcast(F32),
                                   ALU.subtract).then_inc(nat_ready, 1)

            def normalize(b, par):
                pool.wait_ge(rrow_landed, 16 * (b + 1))
                pool.sem_inc(pool_waited, 1)
                pool.partition_broadcast(rsum_all[:], rsum_row[0:1, :], C).then_inc(rall_ready, 1)
                pool.wait_ge(rall_ready, b + 1)
                pool.sem_inc(pool_waited, 1)
                pool.tensor_tensor(u_norm[:, :, par, 0:S], u[0:C, :].rearrange("c (h i) -> c h i", h=H),
                                   rsum_all[:].rearrange("c (h i) -> c h i", h=H), ALU.mult).then_inc(unorm_ready, 1)

            def rstd(pair, n, step):
                pool.wait_ge(out_steps, out_step(pair, step))
                pool.tensor_tensor(rstd2[:], ve2[:], minus_half[:, 0:1], ALU.pow).then_inc(rstd_ready, 1)

            def landing(b, par):
                if isinstance(b, int):
                    return b // 2 + 1
                return landing_of[0]

            landing_of = [None]
            split_context(0, 0)
            pool.wait_ge(nat_ready, 1)
            after(pool, "dve", "ve0")
            done("pool", pool.tensor_tensor(rstd1[:, 0:1], ve1[:, 0:1], minus_half[:, 0:1], ALU.pow), "rstd0")
            after(pool, "dve", "ve")
            done("pool", pool.tensor_tensor(rstd1[:, 1:], ve1[:, 1:], minus_half[:, 1:], ALU.pow), "rstd")
            after(pool, "pool", "rstd")
            split_queries(0, 0)
            pool.memset(cn_hi[1][:, :, C:C + 1].bitcast(F32), 1.0)
            done("pool", pool.memset(cn_lo[1][:, :, C:C + 1].bitcast(F32), 0.0), "ones_nat1")
            after(pool, "pool", "ones_nat1")
            pool.wait_ge(qlo_ready, 1)
            done("pool", pool.memset(ct_hi[1][C:C + 1, :].bitcast(F32), 1.0), "ones1")
            after(pool, "pool", "ones1")
            split_queries(1, 1)
            split_context(1, 1)
            with pool.Fori(0, 3) as k:
                landing_of[0] = k + 2
                split_queries(2 * k + 2, 0)
                normalize(2 * k, 0)
                split_context(2 * k + 2, 0)
                split_queries(2 * k + 3, 1)
                normalize(2 * k + 1, 1)
                split_context(2 * k + 3, 1)
                rstd(k, 0, "ve")
                rstd(k, 1, "ve3")
            normalize(B - 2, 0)
            normalize(B - 1, 1)
            rstd(PAIRS - 1, 0, "ve")
            rstd(PAIRS - 1, 1, "ve3")

        @block.scalar
        def _(act):
            act.dma_start(w_self[:, 1, :], sWk).then_inc(wkq_landed, 16)
            act.dma_start(w_self[:, 0, :], sWq).then_inc(wkq_landed, 16)
            act.dma_start(proj_sb[:], proj.rearrange("(g h) m d -> (h m) g d", g=G)).then_inc(proj_landed, 16)
            act.dma_start(wq_nat[:], xWq).then_inc(xqk_landed, 16)
            act.dma_start(wk_nat[:], xWk).then_inc(xqk_landed, 16)

            def evacuate(dst, name, src, step=None, scale=1.0):
                after(act, "pe", name)
                done("act", act.activation(dst, src, ACT.Copy, scale=scale), step or name)

            def bank(name):
                return banks[FILL_AT[name] % len(banks)]

            evacuate(projT[:], "projT", bank("projT"))
            for n, step in enumerate(("kT", "qT")):
                after(act, "dve", step)
                done("act", act.activation(kq_sq[:, n], kq_scaled[:, n], ACT.Square), f"square{n}")

            def exp_features(n, j):
                after(act, "dve", ("xw", (n, j)))
                done("act", act.activation(phi[:, n, j], phi[:, n, j], ACT.Exp), ("exp", (n, j)))

            exp_features(0, 0)
            evacuate(wT_self[:, 2:4], "wT_vo", bank("wT_vo")[:, 0:256].rearrange("p (n d) -> p n d", n=2))
            after(act, "pool", ("ones", 1))
            for par in range(2):
                rows = slice(SLOT * par, SLOT * par + S)
                src = bank("v").rearrange("p (j g c) -> p j g c", j=PAIRS, g=G)[rows]
                evacuate(v_masked[rows, :, par, :, 0:HG * DK], "v", src, "v" if par else "v0")

            def weight_copy(w, i):
                dst = {"q": wqT, "k": wkT, "v": wvT}[w]
                width = D if w == "q" else C
                src = bank(("wT", (w, i)))[:, 0:4 * width].rearrange("p (n c) -> p n c", n=4)
                evacuate(dst[:, 4 * i:4 * i + 4, :], ("wT", (w, i)), src)

            def qk_copy(i, par):
                dst = wqk[:, 8 * i:8 * i + 8, :].rearrange("p (n two) c -> p two n c", two=2)[:, par]
                src = bank(("wqk", (i, par)))[:, 0:4 * C].rearrange("p (n c) -> p n c", n=4)
                evacuate(dst, ("wqk", (i, par)), src, scale=float(XD) ** -0.5)

            def vo_copy(i, par):
                dst = wvo[:, 8 * i:8 * i + 8, :].rearrange("p (n two) d -> p two n d", two=2)[:, par]
                src = bank(("wvo", (i, par)))[0:C, :].rearrange("p (n d) -> p n d", n=4)
                evacuate(dst, ("wvo", (i, par)), src)

            def context_hi(b, par, slot, unit):
                act.wait_ge(mx_filled, slot + 1)
                act.activation(ct_hi[par][0:C, TW * unit:TW * unit + TW], mx[unit % 2][0:C, 0:TW],
                               ACT.Copy).then_inc(cthi_ready, 1)

            def context_rows_hi(b, par, landed):
                act.wait_ge(ctx_landed[par], 16 * landed)
                wait(act, pv_done, KT * (b - 1))
                act.activation(cn_hi[par][:, :, 0:C], ctx_nat[:, par], ACT.Copy).then_inc(nathi_ready, 1)

            def collect(b):
                act.wait_ge(pv_done, KT * (b + 1))
                wait(act, unorm_ready, b)
                for half in range(2):
                    act.activation(u[:, QH * half:QH * half + QH], acc[0:C + 1, half, 0:QH], ACT.Copy).then_inc(u_ready, 1)

            def tanh(pair, slot, at):
                act.wait_ge(mx_filled, slot + 1)
                act.activation(tanh_g[:], mx[at % 2][:, 0:HID], ACT.Tanh, scale=0.5).then_inc(tanh_ready, 1)

            def work(b, par, base, prep, pair, landed):
                plan = ring_plan(prep, pair is not None)
                number = slots(plan)
                for t in range(KT):
                    g = KT * b + t
                    if (t, 0) in plan and plan[(t, 0)][0] == "transpose":
                        context_hi(b + 1, 1 - par, base + number[(t, 0)], plan[(t, 0)][1])
                    if (t, 0) in plan and plan[(t, 0)][0] == "gate":
                        tanh(pair, base + number[(t, 0)], number[(t, 0)])
                    act.wait_ge(scores_ready, g + 1)
                    wait(act, plo_ready, g - 1)
                    act.activation(p_full[t % 2][:].rearrange("k (s q) -> k s q", s=2), sc[t % 2][0:KP, :, 0:QH],
                                   ACT.Exp).then_inc(p_ready, 1)
                    if (t, 2) in plan and plan[(t, 2)][0] == "transpose":
                        context_hi(b + 1, 1 - par, base + number[(t, 2)], plan[(t, 2)][1])
                    wait(act, pv_done, g - 2)
                    act.activation(p_hi[t % 3][:].rearrange("k (s q) -> k s q", s=2), sc[t % 2][0:KP, :, 0:QH],
                                   ACT.Exp).then_inc(phi_ready, 1)
                    if t == 1 and not (isinstance(b, int) and b == 0):
                        collect(b - 1)
                    if t == 4 and prep:
                        context_rows_hi(b + 1, 1 - par, landed)

            exp_features(0, 1)
            weight_copy("q", 0)
            exp_features(0, 2)
            weight_copy("k", 0)
            exp_features(0, 3)
            qk_copy(0, 0)
            exp_features(1, 0)
            qk_copy(0, 1)
            weight_copy("q", 1)
            exp_features(1, 1)
            weight_copy("k", 1)
            weight_copy("v", 0)
            exp_features(1, 2)
            weight_copy("v", 1)
            qk_copy(1, 0)
            exp_features(1, 3)
            context_hi(0, 0, 0, 0)
            qk_copy(1, 1)
            for unit in range(1, TU):
                context_hi(0, 0, unit, unit)
            for j in PR:
                evacuate(phiqT[:, j], ("phiqT", j), bank(("phiqT", j)).rearrange("p (g s) -> p g s", g=G))
            context_rows_hi(0, 0, 1)

            def merged_copy(j):
                evacuate(mergedT[:, j], ("mergedT", j), bank(("mergedT", j))[:, 0:128])

            merged_copy(0)
            merged_copy(1)
            vo_copy(0, 0)
            merged_copy(2)
            vo_copy(0, 1)
            half = [bank(("q0", i))[0:C, :].rearrange("c (h s) -> c h s", s=SLOT)[:, :, 0:S] for i in range(2)]
            evacuate(q_hi[0][0:C, 0:QH].rearrange("c (h i) -> c h i", i=S), ("q0", 0), half[0], "q0_hi0")
            evacuate(q_all[:, 0, 0:QH].rearrange("c (h i) -> c h i", i=S), ("q0", 0), half[0])
            merged_copy(3)
            after(act, "dve", "q0_hi1")
            evacuate(q_all[:, 0, QH:].rearrange("c (h i) -> c h i", i=S), ("q0", 1), half[1])
            vo_copy(1, 0)
            vo_copy(1, 1)
            for i in range(3):
                src = bank(("ffnT", i))[:, 0:HID].rearrange("p (c n) -> p c n", c=HC)
                evacuate(ffnT[:, i], ("ffnT", i), src)
            for j in PR[1:]:
                evacuate(x1T[:, 128 * j:128 * j + 128], ("x1T", j), bank(("x1T", j))[:, 0:128])
            for h in range(H):
                src = bank(("qk", h))[0:C, 0:(B - 1) * S].rearrange("c (b s) -> c b s", b=B - 1)
                evacuate(q_all[:].rearrange("c b (h i) -> c b h i", h=H)[:, 1:B, h, :], ("qk", h), src)
            sequence_loop(act, work)
            collect(B - 1)
            tanh(PAIRS - 1, LAST_BASE + FINAL.index("gate"), FINAL.index("gate"))

        @block.vector
        def _(dve):
            def bank(name):
                return banks[FILL_AT[name] % len(banks)]

            after(dve, "pe", "xT")
            done("dve", dve.tensor_copy(xT[:], bank("xT")), "xT")
            after(dve, "pe", "wT_kq")
            done("dve", dve.tensor_copy(wT_self[:, 0:2], bank("wT_kq")[:, 0:256].rearrange("p (n d) -> p n d", n=2)),
                 "wT_kq")
            for n, name in enumerate(("kT", "qT")):
                after(dve, "pe", name)
                done("dve", dve.tensor_scalar(kq_scaled[:, n], bank(name), float(DK) ** -0.5, None, ALU.mult), name)

            def context_lo(b, par, slot, unit):
                dve.wait_ge(mx_filled, slot + 1)
                dve.wait_ge(cthi_ready, TU * b + unit + 1)
                cols = slice(TW * unit, TW * unit + TW)
                dve.tensor_tensor(ct_lo[par][:, cols], mx[unit % 2][0:C, 0:TW], ct_hi[par][0:C, cols].bitcast(F32),
                                  ALU.subtract).then_inc(mx_freed, 1)

            def feature_max(n, j):
                name = ("xw", (n, j))
                after(dve, "pe", name)
                xw = bank(name).rearrange("p (h m) -> p h m", h=H)
                done("dve", dve.tensor_reduce(feat_max[:, n, j], xw, AX.X, ALU.max), ("fmax", (n, j)))

            def feature_shift(n, j):
                name = ("xw", (n, j))
                xw = bank(name).rearrange("p (h m) -> p h m", h=H)
                after(dve, "dve", ("fmax", (n, j)))
                done("dve", dve.tensor_tensor(feat_shift[:, n, j], half_sq[:, n, j], feat_max[:, n, j], ALU.add),
                     ("shift", (n, j)))
                after(dve, "dve", ("shift", (n, j)))
                done("dve", dve.tensor_tensor(phi[:, n, j], xw,
                                              feat_shift[:, n, j].unsqueeze(2).broadcast_to([128, H, M]),
                                              ALU.subtract), name)

            def add_eps(n, j):
                after(dve, "act", ("exp", (n, j)))
                done("dve", dve.tensor_scalar(phi[:, n, j], phi[:, n, j], SELF_EPS, None, ALU.add), ("eps", (n, j)))

            for n in range(2):
                feature_max(*XW[n])
                after(dve, "pe", ("norm", n))
                done("dve", dve.tensor_copy(half_sq[:, n], bank(("norm", n))[:, 0:PAIRS * H].rearrange(
                    "p (j h) -> p j h", j=PAIRS)), ("norm", n))
                after(dve, "dve", ("norm", n))
                feature_shift(*XW[n])
            dve.wait_ge(bias_landed, 32)
            dve.wait_ge(x_landed, 32)
            after(dve, "pe", "xT")
            done("dve", dve.tensor_tensor(x_sb[:], x_sb[:], sbo_sb[:].unsqueeze(1).broadcast_to([128, PAIRS, D]),
                                          ALU.add), "xbias")
            for n in XW[2:4]:
                feature_max(*n)
                feature_shift(*n)
            for i in range(4):
                add_eps(*XW[i])
                feature_max(*XW[4 + i])
                feature_shift(*XW[4 + i])
            after(dve, "pool", ("mask", HG - 1))
            for j in PR:
                context_lo(0, 0, j, j)
                after(dve, "pe", ("kv", j))
                src = bank(("kv", j))[:, 0:G * 2 * KVW].rearrange("p (n c) -> p n c", c=KVW)
                done("dve", dve.tensor_tensor(kv[:, j].rearrange("p g s c -> p (g s) c"), src,
                                              block_mask[:].unsqueeze(1).broadcast_to([128, G * 2, KVW]), ALU.mult),
                     ("kv", j))
                add_eps(1, j)

            def self_attention(j):
                after(dve, "pe", ("num", j))
                num = bank(("num", j))[:, 0:G * 2 * KVW].rearrange("p (g s c) -> p g s c", g=G, s=2)
                for par in range(2):
                    rows = slice(SLOT * par, SLOT * par + SLOT)
                    done("dve", dve.tensor_scalar(den[rows, j], num[rows, :, par, HG * DK:], float(M) * SELF_EPS, None,
                                                  ALU.add), ("den" if par else "den0", j))
                after(dve, "dve", ("den", j))
                done("dve", dve.reciprocal(rden[:, j], den[:, j]), ("rden", j))
                after(dve, "dve", ("rden", j))
                for par in range(2):
                    rows = slice(SLOT * par, SLOT * par + SLOT)
                    done("dve", dve.tensor_tensor(
                        merged[rows, j].rearrange("p (g h d) -> p g h d", g=G, h=HG),
                        num[rows, :, par, 0:HG * DK].rearrange("p g (h d) -> p g h d", h=HG),
                        rden[rows, j].unsqueeze(3).broadcast_to([SLOT, G, HG, DK]), ALU.mult),
                        ("num" if par else "num0", j))

            def residual(j):
                after(dve, "pe", ("self", j))
                done("dve", dve.tensor_tensor(y1[:, j], bank(("self", j))[:, 0:D], x_sb[:, j], ALU.add), ("self", j))
                after(dve, "dve", ("self", j))
                done("dve", dve.bn_stats(stats1[:, j], y1[:, j]), ("stats", j))
                after(dve, "dve", ("stats", j))
                done("dve", dve.bn_aggr(mv1[:, j], stats1[:, j]), ("aggr", j))

            def layer_norm(j):
                done("dve", dve.tensor_scalar(x1[:, j], y1[:, j], mv1[:, j, 0:1], rstd1[:, j:j + 1], ALU.subtract,
                                              ALU.mult), ("x1", j))

            self_attention(0)
            self_attention(1)
            self_attention(2)
            residual(0)
            after(dve, "dve", ("aggr", 0))
            done("dve", dve.tensor_scalar(ve1[:, 0:1], mv1[:, 0:1, 1], LN_EPS, None, ALU.add), "ve0")
            self_attention(3)
            residual(1)
            after(dve, "pool", "rstd0")
            layer_norm(0)
            residual(2)
            after(dve, "pe", ("x1T", 0))
            done("dve", dve.tensor_copy(x1T[:, 0:128], bank(("x1T", 0))[:, 0:128]), ("x1T", 0))
            dve.wait_ge(ffn_landed, 48)
            for i in range(3):
                done("dve", dve.tensor_scalar(ffn_nat[:, i], ffn_int[:, i], 1.0 / 127.0, None, ALU.mult), ("ffn", i))
            after(dve, "pe", ("q0", 1))
            done("dve", dve.tensor_copy(q_hi[0][0:C, QH:].rearrange("c (h i) -> c h i", i=S),
                                        bank(("q0", 1))[0:C, :].rearrange("c (h s) -> c h s", s=SLOT)[:, :, 0:S]), "q0_hi1")
            after(dve, "dve", "q0_hi1")
            after(dve, "act", "q0_hi0")
            dve.sem_inc(qhi_ready, 1)
            residual(3)
            after(dve, "dve", ("aggr", PAIRS - 1))
            done("dve", dve.tensor_scalar(ve1[:, 1:], mv1[:, 1:, 1], LN_EPS, None, ALU.add), "ve")

            def chunk_max(slot, at, j, c):
                dve.wait_ge(mx_filled, slot + 1)
                dve.tensor_reduce(max_part[:, j, c:c + 1], mx[at % 2][:, 0:KC], AX.X, ALU.max).then_inc(mx_freed, 1)

            def join_maxima(b, slot):
                dve.wait_ge(mx_freed, slot)
                dve.tensor_reduce(max_neg[:], max_part[:], AX.X, ALU.max, negate=True).then_inc(maxneg_ready, 1)

            def copy_maxima(b, slot, at):
                dve.wait_ge(mx_filled, slot + 1)
                dve.tensor_copy(max_row[:], mx[at % 2][0:QT, 0:128]).then_inc(mx_freed, 1)
                dve.wait_ge(mx_freed, slot + 1)
                dve.sem_inc(maxrow_ready, 1)

            def exp_lo(g, t):
                dve.wait_ge(phi_ready, g + 1)
                wait(dve, pv_done, g - 2)
                dve.tensor_tensor(p_lo[t % 3][:], p_full[t % 2][:], p_hi[t % 3][:].bitcast(F32),
                                  ALU.subtract).then_inc(plo_ready, 1)

            def reciprocals(b):
                dve.wait_ge(sums_landed, 16 * (b + 1))
                dve.reciprocal(rsums[:], sums[:]).then_inc(rsums_ready, 1)

            def step(pair, ins, name):
                ins.then_inc(out_steps, 1)
                dve.wait_ge(out_steps, out_step(pair, name))

            def layer_norm_stats(pair, src, tail):
                dve.bn_stats(stats2[:], src).then_inc(out_steps, 1)
                dve.wait_ge(out_steps, out_step(pair, "stats" + tail))
                dve.sem_inc(dve_waited, 1)
                step(pair, dve.bn_aggr(mv2[:], stats2[:]), "aggr" + tail)
                step(pair, dve.tensor_scalar(ve2[:], mv2[:, 1:2], LN_EPS, None, ALU.add), "ve" + tail)

            def output(what, pair, slot, at):
                src = mx[at % 2]
                dve.wait_ge(mx_filled, slot + 1)
                if what == "out":
                    step(pair, dve.tensor_tensor(y2[:], src[:, 0:D], x1b[:, pair, :], ALU.add), "y2")
                    dve.sem_inc(mx_freed, 1)
                    layer_norm_stats(pair, y2[:], "")
                if what == "x2T":
                    step(pair, dve.tensor_copy(x2T[:], src[:, 0:128]), "x2T")
                    dve.sem_inc(mx_freed, 1)
                if what == "gate":
                    dve.wait_ge(tanh_ready, pair + 1)
                    step(pair, dve.scalar_tensor_tensor(out=silu_g[:], in0=tanh_g[:], scalar=1.0, in1=src[:, 0:HID],
                                                        op0=ALU.add, op1=ALU.mult), "silu")
                    dve.sem_inc(mx_freed, 1)
                if what == "up":
                    step(pair, dve.scalar_tensor_tensor(out=hidT[:].rearrange("p c s -> p (c s)"), in0=silu_g[:],
                                                        scalar=0.5, in1=src[:, 0:HID], op0=ALU.mult, op1=ALU.mult), "hid")
                    dve.sem_inc(mx_freed, 1)
                if what == "down":
                    step(pair, dve.tensor_tensor(y2[:], src[:, 0:D], x2[:], ALU.add), "y3")
                    dve.sem_inc(mx_freed, 2)
                    layer_norm_stats(pair, y2[:], "3")

            def finish_norm(pair, dst, n, name):
                dve.wait_ge(rstd_ready, 2 * pair + n)
                step(pair, dve.tensor_scalar(dst, y2[:], mv2[:, 0:1], rstd2[:], ALU.subtract, ALU.mult), name)

            def queries_hi(b, par):
                wait(dve, scores_ready, KT * (b - 1))
                dve.tensor_copy(q_hi[par][0:C, :], q_all[:, b, :]).then_inc(qhi_ready, 1)

            def work(b, par, base, prep, pair, landed):
                plan = ring_plan(prep, pair is not None)
                number = slots(plan)
                if prep:
                    if isinstance(b, int):
                        after(dve, "act", ("qk", H - 1))
                    queries_hi(b + 1, 1 - par)
                for t in range(KT):
                    for p in range(4):
                        if p == 2 and not (isinstance(b, int) and b == 0 and t == 0):
                            exp_lo(KT * b + t - 1, (t - 1) % KT)
                        if (t, p) not in plan:
                            continue
                        (kind, what), at = plan[(t, p)], number[(t, p)]
                        if kind == "transpose":
                            context_lo(b + 1, 1 - par, base + at, what)
                        elif kind == "max":
                            chunk_max(base + at, at, *what)
                            if what == MAXES[-1]:
                                join_maxima(b + 1, base + at + 1)
                        elif kind == "maxrow":
                            copy_maxima(b + 1, base + at, at)
                        else:
                            output(kind, pair, base + at, at)
                    if t == 3 and not (isinstance(b, int) and b == 0):
                        reciprocals(b - 1)
                    if t == 8 and pair is not None:
                        finish_norm(pair, x2[:], 1, "x2")
                if pair is not None:
                    finish_norm(pair, x3[:, pair, :], 2, "x3")

            for n, (j, c) in enumerate(MAXES):
                chunk_max(TU + n, TU + n, j, c)
                if n == 1:
                    after(dve, "pool", "rstd")
                    for i in PR[1:]:
                        layer_norm(i)
            join_maxima(0, PREP_SLOTS - 1)
            done("dve", dve.tensor_tensor(x1b[:], x1[:], xbo_sb[:].unsqueeze(1).broadcast_to([128, PAIRS, D]),
                                          ALU.add), "x1b")
            copy_maxima(0, PREP_SLOTS - 1, PREP_SLOTS - 1)
            sequence_loop(dve, work)
            exp_lo(KT * B - 1, KT - 1)
            reciprocals(B - 1)
            for n, what in enumerate(FINAL):
                output(what, PAIRS - 1, LAST_BASE + n, n)
                if what == "out":
                    finish_norm(PAIRS - 1, x2[:], 1, "x2")
            finish_norm(PAIRS - 1, x3[:, PAIRS - 1, :], 2, "x3")

        @block.tensor
        def _(pe):
            def fill(name):
                n = FILL_AT[name]
                if n >= len(banks):
                    before, engine = FILLS[n - len(banks)]
                    after(pe, engine, before)
                return banks[n % len(banks)]

            def mm(dst, lhsT, rhs, start=True, stop=True):
                return pe.matmul(dst, lhsT, rhs, start=start, stop=stop, skip_group_check=True)

            after(pe, "pool", "ident")
            pe.wait_ge(x_landed, 32)
            dst = fill("xT")
            for j in PR:
                last = pe.transpose(dst[:, 128 * j:128 * j + 128], x_sb[:, j], ident[:])
            done("pe", last, "xT")
            def self_weights(name, first):
                dst = fill(name)
                for n in range(2):
                    last = pe.transpose(dst[:, 128 * n:128 * n + 128], w_self[:, first + n], ident[:])
                done("pe", last, name)

            pe.wait_ge(wkq_landed, 32)
            self_weights("wT_kq", 0)
            after(pe, "dve", "xT")
            after(pe, "dve", "wT_kq")
            done("pe", mm(fill("kT"), wT_self[:, 1], xT[:]), "kT")
            after(pe, "pool", ("wide", HG - 1))
            dst = fill("projT")
            for g in range(G):
                last = pe.transpose(dst[:, 128 * g:128 * g + 128], proj_wide[:, g].rearrange("p h d -> p (h d)"), ident[:])
            done("pe", last, "projT")
            done("pe", mm(fill("qT"), wT_self[:, 0], xT[:]), "qT")

            def random_features(n, j):
                after(pe, "act", "projT")
                after(pe, "dve", "qT" if n else "kT")
                done("pe", mm(fill(("xw", (n, j))), kq_scaled[:, n, 128 * j:128 * j + 128], projT[:]), ("xw", (n, j)))

            def weight_transposes(w, i):
                src = {"q": wq_nat, "k": wk_nat, "v": wv_nat}[w]
                width = D if w == "q" else C
                dst = fill(("wT", (w, i)))
                for n in range(4):
                    cols = slice(128 * (4 * i + n), 128 * (4 * i + n) + 128)
                    last = pe.transpose(dst[:, width * n:width * n + width], src[:, cols], ident[0:width, 0:width])
                done("pe", last, ("wT", (w, i)))

            def head_products(name, i, par, lhs, rhs, lhs_width, width):
                dst = fill((name, (i, par)))
                rows = slice(XD * par, XD * par + XD)
                for n in range(4):
                    last = mm(dst[0:lhs_width, width * n:width * n + width], lhs[rows, 4 * i + n, :],
                              rhs[rows, 4 * i + n, :])
                done("pe", last, (name, (i, par)))

            def half_norms(n):
                after(pe, "pool", "norm2")
                after(pe, "act", f"square{n}")
                dst = fill(("norm", n))
                for j in PR:
                    last = mm(dst[:, j * H:j * H + H], kq_sq[:, n, 128 * j:128 * j + 128], half_norm[:])
                done("pe", last, ("norm", n))

            random_features(0, 0)
            half_norms(0)
            random_features(0, 1)
            pe.wait_ge(wvo_landed, 32)
            self_weights("wT_vo", 2)
            half_norms(1)
            after(pe, "act", "wT_vo")
            dst = fill("v")
            for j in PR:
                last = mm(dst[:, 128 * j:128 * j + 128], xT[:, 128 * j:128 * j + 128], wT_self[:, 2])
            done("pe", last, "v")

            def ring(slot):
                wait(pe, mx_freed, slot - 1)

            def context_transposes(b, par, slot, unit, landed):
                ring(slot)
                pe.wait_ge(ctx_landed[par], 16 * landed)
                for n in range(KT // TU):
                    last = pe.transpose(mx[unit % 2][0:C, KP * n:KP * n + KP], ctx_nat[:, par, 3 * unit + n],
                                        ident[0:KP, 0:KP])
                last.then_inc(mx_filled, 1)

            def max_scores(b, par, slot, at, j, c):
                ring(slot)
                pe.wait_ge(qhi_ready, b + 1)
                pe.wait_ge(cthi_ready, TU * (b + 1))
                mm(mx[at % 2][:, 0:KC], q_hi[par][0:C, 128 * j:128 * j + 128],
                   ct_hi[par][0:C, KC * c:KC * c + KC]).then_inc(mx_filled, 1)

            def turn_maxima(b, slot, at):
                ring(slot)
                pe.wait_ge(maxneg_ready, b + 1)
                pe.transpose(mx[at % 2][0:QT, 0:128], max_neg[:], ident[:]).then_inc(mx_filled, 1)

            def scores(g, t, par, half):
                dst = sc[t % 2][0:KP, half, 0:QH]
                cols, keys = slice(QH * half, QH * half + QH), slice(t, NCTX, KT)
                keys = slice(KP * t, KP * t + KP)
                mm(dst, ct_hi[par][:, keys], q_hi[par][:, cols], True, False)
                mm(dst, ct_lo[par][:, keys], q_hi[par][0:C, cols], False, False)
                last = mm(dst, ct_hi[par][0:C, keys], q_lo[par][:, cols], False, True)
                if half:
                    last.then_inc(scores_ready, 1)

            def context_sum(t, par, half):
                dst = acc[0:C + 1, half, 0:QH]
                cols = slice(QH * half, QH * half + QH)
                mm(dst, cn_hi[par][:, t], p_hi[t % 3][:, cols], t == 0, False)
                mm(dst, cn_lo[par][:, t], p_hi[t % 3][:, cols], False, False)
                last = mm(dst, cn_hi[par][:, t], p_lo[t % 3][:, cols], False, t == KT - 1)
                if half:
                    last.then_inc(pv_done, 1)

            def output(what, pair, slot, at):
                ring(slot)
                dst = mx[at % 2]
                if what == "out":
                    pe.wait_ge(unorm_ready, 2 * pair + 2)
                    for h in range(H):
                        last = mm(dst[:, 0:D], u_norm[:, h].rearrange("c p s -> c (p s)"), wvo[:, h], h == 0, h == H - 1)
                if what == "x2T":
                    pe.wait_ge(out_steps, out_step(pair, "x2"))
                    last = pe.transpose(dst[:, 0:128], x2[:], ident[:])
                if what in ("gate", "up"):
                    pe.wait_ge(out_steps, out_step(pair, "x2T"))
                    for c in range(HC):
                        last = mm(dst[:, 128 * c:128 * c + 128], ffnT[:, 0 if what == "gate" else 1, c], x2T[:])
                if what == "down":
                    pe.wait_ge(out_steps, out_step(pair, "hid"))
                    for c in range(HC):
                        last = mm(dst[:, 0:D], hidT[:, c], ffnT[:, 2, c], c == 0, c == HC - 1)
                last.then_inc(mx_filled, 2 if what == "down" else 1)

            def sum_step(b, t, par, part):
                if part == 0:
                    pe.wait_ge(plo_ready, KT * b + t + 1)
                    if t == 0:
                        pe.wait_ge(nat_ready, b + 1)
                if t == 0:
                    wait(pe, u_ready, 2 * b - 1 + part if not (isinstance(b, int) and b == 0) else 0)
                context_sum(t, par, part)

            def work(b, par, base, prep, pair, landed):
                plan = ring_plan(prep, pair is not None)
                number = slots(plan)

                def extra(t, p):
                    if (t, p) not in plan:
                        return
                    (kind, what), at = plan[(t, p)], number[(t, p)]
                    if kind == "transpose":
                        context_transposes(b + 1, 1 - par, base + at, what, landed)
                    elif kind == "max":
                        max_scores(b + 1, 1 - par, base + at, at, *what)
                    elif kind == "maxrow":
                        turn_maxima(b + 1, base + at, at)
                    else:
                        output(kind, pair, base + at, at)

                first = isinstance(b, int) and b == 0
                for t in range(KT):
                    extra(t, 0)
                    g = KT * b + t
                    if t == 0:
                        pe.wait_ge(maxrow_landed, 16 * (b + 1))
                        pe.wait_ge(qlo_ready, b + 1)
                    wait(pe, phi_ready, g - 1)
                    scores(g, t, par, 0)
                    extra(t, 1)
                    scores(g, t, par, 1)
                    extra(t, 2)
                    if t >= 2:
                        sum_step(b, t - 2, par, 0)
                    elif not first:
                        sum_step(b - 1, KT + t - 2, 1 - par, 0)
                    extra(t, 3)
                    if t >= 2:
                        sum_step(b, t - 2, par, 1)
                    elif not first:
                        sum_step(b - 1, KT + t - 2, 1 - par, 1)

            def transposed_context(unit):
                context_transposes(0, 0, unit, unit, 1)

            def products_qk(i, par):
                head_products("wqk", i, par, wqT, wkT, D, C)

            def products_vo(i, par):
                head_products("wvo", i, par, wvT, wo_nat, C, D)

            def key_values(j):
                after(pe, "dve", ("eps", (0, j)))
                dst = fill(("kv", j))
                for g in range(G):
                    last = mm(dst[:, 2 * KVW * g:2 * KVW * (g + 1)].rearrange("p (s c) -> p s c", s=2),
                              phi[:, 0, j, HG * g:HG * g + HG, :].rearrange("p h m -> p (h m)"), v_masked[:, j, :, g, :])
                done("pe", last, ("kv", j))

            def turn_phiq(j):
                after(pe, "dve", ("eps", (1, j)))
                dst = fill(("phiqT", j))
                for g in range(G):
                    last = pe.transpose(dst[:, 128 * g:128 * g + 128],
                                        phi[:, 1, j, HG * g:HG * g + HG, :].rearrange("p h m -> p (h m)"), ident[:])
                done("pe", last, ("phiqT", j))

            def numerators(j):
                after(pe, "act", ("phiqT", j))
                after(pe, "dve", ("kv", j))
                dst = fill(("num", j))
                for g in range(G):
                    last = mm(dst[:, 2 * KVW * g:2 * KVW * (g + 1)], phiqT[:, j, g, :],
                              kv[:, j, g].rearrange("p s c -> p (s c)"))
                done("pe", last, ("num", j))

            def x1_transpose(j):
                after(pe, "dve", ("x1", j))
                done("pe", pe.transpose(fill(("x1T", j))[:, 0:128], x1[:, j], ident[:]), ("x1T", j))

            def turn_merged(j):
                after(pe, "dve", ("num", j))
                done("pe", pe.transpose(fill(("mergedT", j))[:, 0:128], merged[:, j], ident[:]), ("mergedT", j))

            def project(j):
                after(pe, "act", ("mergedT", j))
                done("pe", mm(fill(("self", j))[:, 0:D], mergedT[:, j], wT_self[:, 3]), ("self", j))

            random_features(0, 2)
            pe.wait_ge(xqk_landed, 32)
            weight_transposes("q", 0)
            random_features(0, 3)
            weight_transposes("k", 0)
            random_features(1, 0)
            after(pe, "act", ("wT", ("k", 0)))
            products_qk(0, 0)
            random_features(1, 1)
            products_qk(0, 1)
            weight_transposes("q", 1)
            random_features(1, 2)
            weight_transposes("k", 1)
            pe.wait_ge(xvo_landed, 32)
            weight_transposes("v", 0)
            random_features(1, 3)
            weight_transposes("v", 1)
            after(pe, "act", ("wT", ("k", 1)))
            products_qk(1, 0)
            transposed_context(0)
            after(pe, "act", "v")
            key_values(0)
            transposed_context(1)
            products_qk(1, 1)
            key_values(1)
            key_values(2)
            transposed_context(2)
            key_values(3)
            transposed_context(3)
            turn_phiq(0)
            turn_phiq(1)
            numerators(0)
            turn_phiq(2)
            numerators(1)
            turn_phiq(3)
            numerators(2)
            turn_merged(0)
            numerators(3)
            project(0)
            turn_merged(1)
            after(pe, "act", ("wT", ("v", 1)))
            products_vo(0, 0)
            project(1)
            turn_merged(2)
            products_vo(0, 1)
            project(2)
            x1_transpose(0)
            after(pe, "dve", ("x1T", 0))
            after(pe, "act", ("wqk", AB[-1]))
            for i in range(2):
                dst = fill(("q0", i))
                for h in range(8):
                    last = mm(dst[0:C, SLOT * h:SLOT * h + SLOT], wqk[:, 8 * i + h], x1T[:, 0:SLOT])
                done("pe", last, ("q0", i))
            turn_merged(3)
            products_vo(1, 0)
            project(3)
            after(pe, "pool", "ones0")

            def first_maxima(n):
                max_scores(0, 0, TU + n, TU + n, *MAXES[n])

            first_maxima(0)
            products_vo(1, 1)
            for i in range(3):
                first_maxima(1 + i)
                after(pe, "dve", ("ffn", i))
                dst = fill(("ffnT", i))
                for c in range(HC):
                    last = pe.transpose(dst[:, 128 * c:128 * c + 128], ffn_nat[:, i, c], ident[:])
                done("pe", last, ("ffnT", i))
            for j in PR[1:]:
                x1_transpose(j)
            first_maxima(4)
            after(pe, "act", ("x1T", PAIRS - 1))
            others = x1T[:].rearrange("p (b s) -> p b s", b=B)[:, 1:B, 0:S]

            def other_queries(h):
                dst = fill(("qk", h))[0:C, 0:(B - 1) * S].rearrange("c (b s) -> c b s", b=B - 1)
                done("pe", mm(dst, wqk[:, h], others), ("qk", h))

            late = 3
            begun, early = 5, H - late
            for n in range(len(MAXES) - begun):
                for h in range(early * n // (len(MAXES) - begun), early * (n + 1) // (len(MAXES) - begun)):
                    other_queries(h)
                first_maxima(begun + n)
            other_queries(H - late)
            turn_maxima(0, PREP_SLOTS - 1, PREP_SLOTS - 1)
            for h in range(H - late + 1, H):
                other_queries(h)
            after(pe, "act", ("qk", H - 1))

            sequence_loop(pe, work)
            for t in (KT - 2, KT - 1):
                for half in range(2):
                    sum_step(B - 1, t, 1, half)
            for n, what in enumerate(FINAL):
                output(what, PAIRS - 1, LAST_BASE + n, n)


_INS = ['x', 'ctx_768', 'L0_attn_Wq', 'L0_attn_Wk', 'L0_attn_Wv', 'L0_attn_Wo', 'L0_attn_bo', 'L0_attn_proj',
        'L0_xattn_Wq', 'L0_xattn_Wk', 'L0_xattn_Wv', 'L0_xattn_Wo', 'L0_xattn_bo',
        'L0_ffn_w_gate', 'L0_ffn_w_up', 'L0_ffn_w_down']
_OUTS = [((B, S, D), 'float32')]


def kernel(**inputs):
    import numpy as _np
    import concourse.bacc as _bacc
    from concourse import mybir as _mybir
    from concourse.bass_utils import run_bass_kernel_spmd as _run

    nc = _bacc.Bacc("TRN2", target_bir_lowering=False, num_devices=1)
    arrays, args = {}, []
    for name in _INS:
        a = _np.ascontiguousarray(inputs[name])
        arrays[f"in_{name}_dram"] = a
        args.append(nc.dram_tensor(f"in_{name}_dram", a.shape, _mybir.dt.from_np(a.dtype), kind="ExternalInput").ap())
    for i, (shape, dtype) in enumerate(_OUTS):
        dt = _mybir.dt.from_np(_np.dtype(dtype))
        args.append(nc.dram_tensor(f"out_{i}_dram", shape, dt, kind="ExternalOutput").ap())
    program(nc, *args)
    r = _run(nc, [arrays], core_ids=[0])
    got = tuple(r.results[0][f"out_{i}_dram"] for i in range(len(_OUTS)))
    return got[0]
```

```python
from contextlib import ExitStack

import concourse.bass as bass
from concourse import mybir

F32 = mybir.dt.float32
F32R = mybir.dt.float32r
I32 = mybir.dt.int32
ALU = mybir.AluOpType
ACT = mybir.ActivationFunctionType
AX = mybir.AxisListType

B, S, D = 8, 56, 128
SLOT = 64
PAIRS = B // 2
H = 16
DK = D // H
M = 32
G = 4
HG = H // G
KVW = HG * DK + HG
SELF_EPS = 1e-6
C, NCTX = 96, 1500
KT, KP = 12, 125
XD = 64
Q = H * S
QH = Q // 2
QT = Q // 128
KC = NCTX // 3
TU = 4
TW = NCTX // TU
HID = 384
HC = HID // 128
LN_EPS = 1e-5
SUM_P = 112

MAXES = [(j, c) for c in range(3) for j in range(QT)]


def ring_plan(prep, output):
    plan = {}
    if prep:
        for u, at in enumerate([(0, 0), (0, 2), (1, 0), (1, 2)]):
            plan[at] = ("transpose", u)
        places = sorted([(t, p) for t in range(2, 10) for p in (1, 3)] + [(t, 2) for t in range(2, 7)])
        for at, what in zip(places, MAXES):
            plan[at] = ("max", what)
        plan[(10, 3)] = ("maxrow", None)
    if output:
        plan[(7, 2)] = ("out", None)
        plan[(9, 2)] = ("x2T", None)
        plan[(10, 0)] = ("gate", None)
        plan[(10, 1)] = ("up", None)
        plan[(11, 2)] = ("down", None)
    return plan


PREP_SLOTS = 26
OUT_SLOTS = 6


def program(nc, x, ctx_in, sWq, sWk, sWv, sWo, sbo, proj, xWq, xWk, xWv, xWo, xbo, w_gate, w_up, w_down, out):
    with ExitStack() as stack:
        def sb(name, shape, dt=F32):
            return stack.enter_context(nc.sbuf_tensor(name, shape, dt))

        def ps(name, shape):
            return stack.enter_context(nc.psum_tensor(name, shape, F32))

        def sem(name):
            return stack.enter_context(nc.semaphore(name))

        ident = sb("ident", [128, 128])
        block_mask = sb("block_mask", [128, KVW])
        half_norm = sb("half_norm", [128, H])
        minus_half = sb("minus_half", [128, PAIRS])
        wT_self = sb("wT_self", [128, 4, 128])
        proj_sb = sb("proj_sb", [128, G, DK])
        sbo_sb = sb("sbo_sb", [128, D])
        xbo_sb = sb("xbo_sb", [128, D])
        wqk = sb("wqk", [128, H, C])
        wvo = sb("wvo", [C, H, D])
        ffnT = sb("ffnT", [128, 3, HC, 128])

        x_sb = sb("x_sb", [128, PAIRS, D])
        half_sq = sb("half_sq", [128, 2, PAIRS, H])
        feat_max = sb("feat_max", [128, 2, PAIRS, H])
        feat_shift = sb("feat_shift", [128, 2, PAIRS, H])
        den = sb("den", [128, PAIRS, G, HG])
        rden = sb("rden", [128, PAIRS, G, HG])
        merged = sb("merged", [128, PAIRS, D])
        mergedT = sb("mergedT", [128, PAIRS, D])
        y1 = sb("y1", [128, PAIRS, D])
        stats1 = sb("stats1", [128, PAIRS, 6])
        mv1 = sb("mv1", [128, PAIRS, 2])
        ve1 = sb("ve1", [128, PAIRS])
        rstd1 = sb("rstd1", [128, PAIRS])
        x1 = sb("x1", [128, PAIRS, D])
        x1b = sb("x1b", [128, PAIRS, D])
        x1T = sb("x1T", [128, SLOT])

        q_all = sb("q_all", [C, B, Q])
        ctx_nat = sb("ctx_nat", [KP, 2, KT, C])
        cn_hi = [sb("cn_hi0", [KP, KT, C + 1], F32R)]
        cn_lo = [sb("cn_lo0", [KP, KT, C + 1], F32R)]
        ct_hi = [sb("ct_hi0", [C + 1, NCTX], F32R)]
        ct_lo = [sb("ct_lo0", [C, NCTX], F32R)]
        q_hi = [sb("q_hi0", [C + 1, Q], F32R)]
        q_lo = [sb("q_lo0", [C, Q], F32R)]
        max_part = sb("max_part", [128, QT, 3])
        max_neg = sb("max_neg", [128, QT])
        max_row = sb("max_row", [QT, 128], F32R)
        sums = sb("sums", [SUM_P, Q // SUM_P])
        rsums = sb("rsums", [SUM_P, Q // SUM_P])
        u_norm = sb("u_norm", [C, H, 2, SLOT])

        stats2 = sb("stats2", [128, 6])
        mv2 = sb("mv2", [128, 2])
        ve2 = sb("ve2", [128, 1])
        rstd2 = sb("rstd2", [128, 1])
        x3 = sb("x3", [128, PAIRS, D])

        last_recip = sb("last_recip", [SUM_P, Q // SUM_P])

        setup_only = ExitStack()

        def early(name, shape, dt=F32):
            return setup_only.enter_context(nc.sbuf_tensor(name, shape, dt))

        v_masked = early("v_masked", [128, PAIRS, 2, G, KVW])
        phi = early("phi", [128, 2, PAIRS, H, M])
        kv = early("kv", [128, PAIRS, G, 2, KVW])
        phiqT = early("phiqT", [128, PAIRS, G, 128])
        wq_nat = early("wq_nat", [128, H * XD])
        wk_nat = early("wk_nat", [C, H * XD])
        wv_nat = early("wv_nat", [C, H * XD])
        wo_nat = early("wo_nat", [128, 8, D])
        wqT = early("wqT", [128, 8, D])
        wkT = early("wkT", [128, 8, C])
        wvT = early("wvT", [128, 8, C])
        xT = early("xT", [128, 512])
        ffn_int = early("ffn_int", [128, 3, HC, 128], I32)
        ffn_nat = early("ffn_nat", [128, 3, HC, 128])
        w_self = early("w_self", [128, 4, 128])
        features_only = ExitStack()
        proj_wide, projT, kq_scaled, kq_sq = [
            features_only.enter_context(nc.sbuf_tensor(name, shape, F32)) for name, shape in
            (("proj_wide", [128, G, H, DK]), ("projT", [128, 512]), ("kq_scaled", [128, 2, 512]), ("kq_sq", [128, 2, 512]))]
        features_only.close()
        wqk_hi = early("wqk_hi", [128, H, C], F32R)
        wqk_lo = early("wqk_lo", [128, H, C], F32R)
        x1T_hi = early("x1T_hi", [128, B - 1, S], F32R)
        x1T_lo = early("x1T_lo", [128, B - 1, S], F32R)
        setup_only.close()
        for pair_of, name, shape in (
                (cn_hi, "cn_hi1", [KP, KT, C + 1]), (cn_lo, "cn_lo1", [KP, KT, C + 1]), (ct_hi, "ct_hi1", [C + 1, NCTX]),
                (ct_lo, "ct_lo1", [C, NCTX]), (q_hi, "q_hi1", [C + 1, Q]), (q_lo, "q_lo1", [C, Q])):
            pair_of.append(sb(name, shape, F32R))
        p_full = [sb(f"p_full{i}", [KP, Q]) for i in range(2)]
        p_hi = [sb(f"p_hi{i}", [KP, Q], F32R) for i in range(3)]
        p_lo = [sb(f"p_lo{i}", [KP, Q], F32R) for i in range(3)]
        u = sb("u", [C + 1, Q])
        rsum_row = sb("rsum_row", [1, Q])
        rsum_all = sb("rsum_all", [C, Q])
        y2 = sb("y2", [128, D])
        x2 = sb("x2", [128, D])
        x2T = sb("x2T", [128, 128])
        tanh_g = sb("tanh_g", [128, HID])
        silu_g = sb("silu_g", [128, HID])
        hidT = sb("hidT", [128, HC, 128])

        sc = [ps(f"sc{i}", [128, 2, 512]) for i in range(2)]
        acc = ps("acc", [128, 2, 512])
        mx = [ps(f"mx{i}", [128, 512]) for i in range(2)]
        banks = [sc[0][:, 0, :], sc[0][:, 1, :], sc[1][:, 0, :], sc[1][:, 1, :],
                 acc[:, 0, :], acc[:, 1, :]]

        PR = range(PAIRS)
        HEADS4 = [(i, par) for i in range(2) for par in range(2)]
        def xw(n, j):
            return ("xw", (n, j)), "dve"

        def wt(w, i):
            return ("wT", (w, i)), "act"

        def of_heads(name, i, par):
            return (name, (i, par)), "act"

        def act_(name, i):
            return (name, i), "act"

        def dve_(name, i):
            return (name, i), "dve"

        FILLS = ([("xT", "dve"), ("wT_kq", "dve"), ("kT", "dve"), ("projT", "act"), ("qT", "dve"), xw(0, 0),
                  dve_("norm", 0), xw(1, 0), dve_("norm", 1), ("wT_vo", "act"), ("v", "act"),
                  xw(0, 1), wt("q", 0), xw(1, 1), dve_("kv", 0), wt("k", 0), act_("phiqT", 0), xw(0, 2),
                  of_heads("wqk", 0, 0), dve_("num", 0), xw(1, 2), wt("q", 1), act_("mergedT", 0),
                  of_heads("wqk", 0, 1), dve_("kv", 1), act_("phiqT", 1), dve_("self", 0), xw(0, 3), wt("k", 1),
                  dve_("num", 1), xw(1, 3), of_heads("wqk", 1, 0), of_heads("wqk", 1, 1), dve_("x1T", 0),
                  dve_("kv", 2), act_("mergedT", 1), dve_("self", 1), act_("phiqT", 2), act_("q0", 0),
                  act_("q0", 1), dve_("num", 2), dve_("kv", 3), act_("phiqT", 3), wt("v", 0), act_("mergedT", 2), dve_("num", 3),
                  dve_("self", 2), wt("v", 1), act_("mergedT", 3)]
                 + [of_heads("wvo", 0, 0), dve_("self", 3), of_heads("wvo", 0, 1), of_heads("wvo", 1, 0),
                    of_heads("wvo", 1, 1)]
                 + [dve_("x1T", j) for j in PR[1:]] + [act_("ffnT", i) for i in range(3)]
                 + [act_("qk", h) for h in range(H)])
        FILL_AT = {name: i for i, (name, _) in enumerate(FILLS)}

        ACT_SETUP = (["projT", "square0", "square1", ("exp", (0, 0)), "wT_vo", ("exp", (1, 0)), "v0", "v",
                      ("wT", ("q", 0)), ("exp", (0, 1)), ("wT", ("k", 0)), ("phiqT", 0), ("exp", (1, 1)), ("wqk", (0, 0)),
                      ("exp", (0, 2)), ("wT", ("q", 1)), ("mergedT", 0), ("wqk", (0, 1)), ("phiqT", 1),
                      ("exp", (1, 2)), ("wT", ("k", 1)), ("exp", (0, 3)), ("wqk", (1, 0)), ("wqk", (1, 1)),
                      ("exp", (1, 3)), ("x1T_hi", 0), ("mergedT", 1), ("phiqT", 2), "q0_hi0", ("q0", 0), ("q0", 1),
                      ("phiqT", 3), ("wT", ("v", 0)), ("mergedT", 2), ("wT", ("v", 1)), ("mergedT", 3),
                      ("wvo", (0, 0)), ("wvo", (0, 1)), ("wvo", (1, 0)), ("wvo", (1, 1))]
                     + [("x1T_hi", j) for j in PR[1:]] + [("ffnT", i) for i in range(3)]
                     + [("qk", h) for h in range(H)])

        def numerator_steps(j):
            return [("den0", j), ("den", j), ("rden", j), ("num0", j), ("num", j)]

        def residual_steps(j):
            return [("self", j), ("stats", j), ("aggr", j)]

        def feature_steps(n, j):
            return [("fmax", (n, j))] + ([("norm", n)] if j == 0 else []) + [("shift", (n, j)), ("xw", (n, j))]

        DVE_SETUP = (["xT", "wT_kq", "kT", "qT"]
                     + feature_steps(0, 0) + feature_steps(1, 0) + feature_steps(0, 1) + feature_steps(1, 1) + [("kv", 0)]
                     + feature_steps(0, 2) + numerator_steps(0) + feature_steps(1, 2) + [("kv", 1)]
                     + residual_steps(0) + ["ve0"] + feature_steps(0, 3) + [("x1", 0)] + numerator_steps(1)
                     + feature_steps(1, 3) + ["x1T_first", ("kv", 2), "wqk_hi"]
                     + residual_steps(1) + [("x1T", 0), "q0_hi1"]
                     + numerator_steps(2) + [("kv", 3)] + numerator_steps(3)
                     + residual_steps(2) + residual_steps(3)
                     + ["ve"] + [("x1", j) for j in PR[1:]] + [("x1T", j) for j in PR[1:]] + ["x1b"])
        POOL_SETUP = (["x_zero", "ident0", "ident", "wide_zero", "norm0", "norm1", "norm2", "mask0", "v_zero",
                       "minus_half"] + [("wide", hl) for hl in range(HG)] + [("mask", hl) for hl in range(HG)]
                      + [("ones", 0), ("ones", 1), "unorm_zero", "ones_nat0", "ones0"]
                      + [("eps", 0), ("eps", 1), "xbias", ("eps", 2), "rstd0", ("eps", 3)] + [("ffn", i) for i in range(3)]
                      + ["wqk_lo", "rstd", "ones_nat1", "ones1"])
        setup = {"act": sem("act_setup"), "dve": sem("dve_setup"), "pool": sem("pool_setup"), "pe": sem("pe_setup")}
        ORDER = {"act": ACT_SETUP, "dve": DVE_SETUP, "pool": POOL_SETUP, "pe": [n for n, _ in FILLS]}
        COUNT = {e: {n: i + 1 for i, n in enumerate(names)} for e, names in ORDER.items()}
        said = {e: 0 for e in ORDER}

        def done(engine, ins, name):
            assert ORDER[engine][said[engine]] == name, (engine, name, ORDER[engine][said[engine]])
            said[engine] += 1
            ins.then_inc(setup[engine], 1)

        def after(eng, engine, name):
            eng.wait_ge(setup[engine], COUNT[engine][name])

        x_landed = sem("x_landed")
        wkq_landed = sem("wkq_landed")
        wvo_landed = sem("wvo_landed")
        xqk_landed = sem("xqk_landed")
        proj_landed = sem("proj_landed")
        bias_landed = sem("bias_landed")
        xvo_landed = sem("xvo_landed")
        ffn_landed = sem("ffn_landed")
        ctx_landed = [sem(f"ctx_landed{i}") for i in range(2)]
        scores_ready = sem("scores_ready")
        phi_ready = sem("phi_ready")
        plo_ready = sem("plo_ready")
        pv_done = sem("pv_done")
        u_ready = sem("u_ready")
        mx_filled = sem("mx_filled")
        mx_freed = sem("mx_freed")
        cthi_ready = sem("cthi_ready")
        qhi_ready = sem("qhi_ready")
        qlo_ready = sem("qlo_ready")
        nathi_ready = sem("nathi_ready")
        nat_ready = sem("nat_ready")
        maxneg_ready = sem("maxneg_ready")
        maxrow_ready = sem("maxrow_ready")
        maxrow_landed = sem("maxrow_landed")
        sums_landed = sem("sums_landed")
        rsums_ready = sem("rsums_ready")
        rrow_landed = sem("rrow_landed")
        rall_ready = sem("rall_ready")
        unorm_ready = sem("unorm_ready")
        out_steps = sem("out_steps")
        rstd_ready = sem("rstd_ready")
        tanh_ready = sem("tanh_ready")
        sums_turned = sem("sums_turned")
        recip_ready = sem("recip_ready")
        recip_spread = sem("recip_spread")
        last_norm = sem("last_norm")
        stored = sem("stored")

        OUT_STEPS = ["y2", "stats", "aggr", "ve", "x2", "x2T", "silu", "hid", "y3", "stats3", "aggr3", "ve3", "x3"]

        def out_step(pair, name):
            return len(OUT_STEPS) * pair + OUT_STEPS.index(name) + 1

        block = stack.enter_context(nc.Block())

        def slots(plan):
            n, number = 0, {}
            for at in sorted(plan):
                number[at] = n
                n += 2 if plan[at][0] == "down" else 1
            return number

        def sequence_loop(eng, work):
            work(0, 0, PREP_SLOTS, True, None, 1)
            with eng.Fori(0, 3) as k:
                per = 2 * PREP_SLOTS + OUT_SLOTS
                work(2 * k + 1, 1, per * k + 2 * PREP_SLOTS, True, None, k + 2)
                work(2 * k + 2, 0, per * k + 3 * PREP_SLOTS, True, k, k + 2)
            work(B - 1, 1, 3 * (2 * PREP_SLOTS + OUT_SLOTS) + 2 * PREP_SLOTS, False, None, None)

        LAST_BASE = 3 * (2 * PREP_SLOTS + OUT_SLOTS) + 2 * PREP_SLOTS
        FINAL = ["out", "x2T", "gate", "up", "down"]

        def wait(eng, s, value):
            if isinstance(value, int) and value <= 0:
                return
            eng.wait_ge(s, value)

        pool_waited = sem("pool_waited")
        dve_waited = sem("dve_waited")

        @block.sync
        def _(sp):
            after(sp, "pool", "x_zero")
            for par in range(2):
                sp.dma_start(x_sb[SLOT * par:SLOT * par + S, :, :],
                             x.rearrange("(j p) i d -> p i j d", p=2)[par]).then_inc(x_landed, 16)
            sp.dma_start(w_self[:, 2, :], sWv).then_inc(wvo_landed, 16)
            sp.dma_start(w_self[:, 3, :], sWo).then_inc(wvo_landed, 16)
            sp.dma_start(wv_nat[:], xWv).then_inc(xvo_landed, 16)
            sp.dma_start(wo_nat[:], xWo.rearrange("(n p) d -> p n d", p=128)).then_inc(xvo_landed, 16)
            for dst, bias in ((sbo_sb, sbo), (xbo_sb, xbo)):
                sp.dma_start(dst[:], bias.rearrange("(a d) -> a d", a=1).broadcast_to([128, D])).then_inc(bias_landed, 16)
            for b in range(2):
                sp.dma_start(ctx_nat[:, b], ctx_in[b].rearrange("(p t) c -> p t c", t=KT)).then_inc(ctx_landed[b], 16)
            sp.dma_start(ffn_int[:, 0], w_gate.rearrange("(c p) d -> p c d", p=128)).then_inc(ffn_landed, 16)
            sp.dma_start(ffn_int[:, 1], w_up.rearrange("(c p) d -> p c d", p=128)).then_inc(ffn_landed, 16)
            sp.dma_start(ffn_int[:, 2], w_down.rearrange("p (c h) -> p c h", c=HC)).then_inc(ffn_landed, 16)

            def place_maxima(par):
                sp.dma_start(q_hi[par][C:C + 1, :].rearrange("a (j q) -> a j q", j=QT).bitcast(F32),
                             max_row[:, :].bitcast(F32)).then_inc(maxrow_landed, 16)

            def work(b, par, load):
                if load:
                    wait(sp, cthi_ready, TU * (b + 1))
                    wait(sp, nat_ready, b + 1)
                    src = ctx_in[b + 2].rearrange("(p t) c -> p t c", t=KT)
                    sp.dma_start(ctx_nat[:, par], src).then_inc(ctx_landed[par], 16)
                sp.wait_ge(maxrow_ready, b + 2)
                place_maxima(1 - par)
                sp.wait_ge(u_ready, 2 * b + 2)
                sp.dma_start(sums[:], u[C:C + 1, :].rearrange("a (p n) -> a p n", p=SUM_P)).then_inc(sums_landed, 16)
                sp.wait_ge(rsums_ready, b + 1)
                sp.dma_start(rsum_row[0:1, :].rearrange("a (p n) -> a p n", p=SUM_P), rsums[:]).then_inc(rrow_landed, 16)

            sp.wait_ge(maxrow_ready, 1)
            place_maxima(0)
            with sp.Fori(0, 3) as k:
                work(2 * k, 0, True)
                work(2 * k + 1, 1, True)
            work(B - 2, 0, False)
            pairs_out = out.rearrange("(j p) i d -> p i j d", p=2)
            sp.wait_ge(out_steps, out_step(PAIRS - 2, "x3"))
            for par in range(2):
                sp.dma_start(pairs_out[par, :, 0:PAIRS - 1],
                             x3[SLOT * par:SLOT * par + S, 0:PAIRS - 1, :]).then_inc(stored, 16)
            sp.wait_ge(out_steps, out_step(PAIRS - 1, "x3"))
            sp.dma_start(pairs_out[0, :, PAIRS - 1], x3[0:S, PAIRS - 1, :]).then_inc(stored, 16)
            sp.wait_ge(stored, 64)

        @block.gpsimd
        def _(pool):
            done("pool", pool.memset(x_sb[:], 0.0), "x_zero")
            done("pool", pool.memset(ident[:], 0.0), "ident0")
            after(pool, "pool", "ident0")
            done("pool", pool.affine_select(out=ident[:], in_=ident[:], compare_op=ALU.not_equal, fill=1.0, base=0,
                                            pattern=[[-1, 128]], channel_multiplier=1), "ident")
            done("pool", pool.memset(proj_wide[:], 0.0), "wide_zero")
            done("pool", pool.memset(half_norm[:], 0.5), "norm0")
            after(pool, "pool", "norm0")
            done("pool", pool.affine_select(out=half_norm[:], in_=half_norm[:], compare_op=ALU.is_ge, fill=0.0, base=0,
                                            pattern=[[-DK, H]], channel_multiplier=1), "norm1")
            after(pool, "pool", "norm1")
            done("pool", pool.affine_select(out=half_norm[:], in_=half_norm[:], compare_op=ALU.is_ge, fill=0.0, base=DK - 1,
                                            pattern=[[DK, H]], channel_multiplier=-1), "norm2")
            done("pool", pool.memset(block_mask[:], 0.0), "mask0")
            done("pool", pool.memset(v_masked[:], 0.0), "v_zero")
            done("pool", pool.memset(minus_half[:], -0.5), "minus_half")
            pool.wait_ge(proj_landed, 16)
            for hl in range(HG):
                rows = slice(M * hl, M * hl + M)
                after(pool, "pool", ("wide", hl - 1) if hl else "minus_half")
                for g in range(G):
                    last = pool.tensor_copy(proj_wide[rows, g, HG * g + hl, :], proj_sb[rows, g, :])
                done("pool", last, ("wide", hl))
            for hl in range(HG):
                rows = slice(M * hl, M * hl + M)
                after(pool, "pool", ("mask", hl - 1) if hl else ("wide", HG - 1))
                pool.memset(block_mask[rows, DK * hl:DK * hl + DK], 1.0)
                done("pool", pool.memset(block_mask[rows, HG * DK + hl:HG * DK + hl + 1], 1.0), ("mask", hl))
            for par in range(2):
                after(pool, "pool", ("ones", par - 1) if par else ("mask", HG - 1))
                for j in PR:
                    last = pool.memset(v_masked[SLOT * par:SLOT * par + S, j, par, :, HG * DK:], 1.0)
                done("pool", last, ("ones", par))
            after(pool, "pool", ("ones", 1))
            done("pool", pool.memset(u_norm[:], 0.0), "unorm_zero")
            pool.memset(cn_hi[0][:, :, C:C + 1].bitcast(F32), 1.0)
            done("pool", pool.memset(cn_lo[0][:, :, C:C + 1].bitcast(F32), 0.0), "ones_nat0")
            after(pool, "pool", "ones_nat0")
            done("pool", pool.memset(ct_hi[0][C:C + 1, :].bitcast(F32), 1.0), "ones0")
            after(pool, "pool", "ones0")
            def keys_eps(j):
                after(pool, "act", ("exp", (0, j)))
                done("pool", pool.tensor_scalar(phi[:, 0, j], phi[:, 0, j], SELF_EPS, None, ALU.add), ("eps", j))

            keys_eps(0)
            keys_eps(1)
            pool.wait_ge(bias_landed, 32)
            pool.wait_ge(x_landed, 32)
            after(pool, "pe", "xT")
            done("pool", pool.tensor_tensor(x_sb[:], x_sb[:], sbo_sb[:].unsqueeze(1).broadcast_to([128, PAIRS, D]),
                                            ALU.add), "xbias")
            keys_eps(2)
            after(pool, "dve", "ve0")
            done("pool", pool.tensor_tensor(rstd1[:, 0:1], ve1[:, 0:1], minus_half[:, 0:1], ALU.pow), "rstd0")
            keys_eps(3)
            pool.wait_ge(ffn_landed, 48)
            for i in range(3):
                done("pool", pool.tensor_scalar(ffn_nat[:, i], ffn_int[:, i], 1.0 / 127.0, None, ALU.mult), ("ffn", i))
            after(pool, "dve", "wqk_hi")
            done("pool", pool.tensor_tensor(wqk_lo[:], wqk[:], wqk_hi[:].bitcast(F32), ALU.subtract), "wqk_lo")

            def split_queries(b, par):
                pool.wait_ge(qhi_ready, b + 1)
                if isinstance(b, int) and b == 0:
                    after(pool, "act", ("q0", 1))
                pool.sem_inc(pool_waited, 1)
                pool.tensor_tensor(q_lo[par][:], q_all[:, b, :], q_hi[par][0:C, :].bitcast(F32),
                                   ALU.subtract).then_inc(qlo_ready, 1)

            def split_context(b, par):
                pool.wait_ge(ctx_landed[par], 16 * landing(b, par))
                pool.wait_ge(nathi_ready, b + 1)
                pool.sem_inc(pool_waited, 1)
                pool.tensor_tensor(cn_lo[par][:, :, 0:C], ctx_nat[:, par], cn_hi[par][:, :, 0:C].bitcast(F32),
                                   ALU.subtract).then_inc(nat_ready, 1)

            def normalize(b, par):
                pool.wait_ge(rrow_landed, 16 * (b + 1))
                pool.sem_inc(pool_waited, 1)
                pool.partition_broadcast(rsum_all[:], rsum_row[0:1, :], C).then_inc(rall_ready, 1)
                pool.wait_ge(rall_ready, b + 1)
                pool.sem_inc(pool_waited, 1)
                pool.tensor_tensor(u_norm[:, :, par, 0:S], u[0:C, :].rearrange("c (h i) -> c h i", h=H),
                                   rsum_all[:].rearrange("c (h i) -> c h i", h=H), ALU.mult).then_inc(unorm_ready, 1)

            def rstd(pair, n, step):
                pool.wait_ge(out_steps, out_step(pair, step))
                pool.tensor_tensor(rstd2[:], ve2[:], minus_half[:, 0:1], ALU.pow).then_inc(rstd_ready, 1)

            def landing(b, par):
                if isinstance(b, int):
                    return b // 2 + 1
                return landing_of[0]

            pool.sem_inc(unorm_ready, 1)
            landing_of = [None]
            after(pool, "dve", "ve")
            done("pool", pool.tensor_tensor(rstd1[:, 1:], ve1[:, 1:], minus_half[:, 1:], ALU.pow), "rstd")
            after(pool, "pool", "rstd")
            split_context(0, 0)
            split_queries(0, 0)
            pool.memset(cn_hi[1][:, :, C:C + 1].bitcast(F32), 1.0)
            done("pool", pool.memset(cn_lo[1][:, :, C:C + 1].bitcast(F32), 0.0), "ones_nat1")
            after(pool, "pool", "ones_nat1")
            pool.wait_ge(qlo_ready, 1)
            done("pool", pool.memset(ct_hi[1][C:C + 1, :].bitcast(F32), 1.0), "ones1")
            after(pool, "pool", "ones1")
            split_queries(1, 1)
            split_context(1, 1)
            with pool.Fori(0, 3) as k:
                landing_of[0] = k + 2
                split_queries(2 * k + 2, 0)
                normalize(2 * k, 0)
                split_context(2 * k + 2, 0)
                split_queries(2 * k + 3, 1)
                normalize(2 * k + 1, 1)
                split_context(2 * k + 3, 1)
                rstd(k, 0, "ve")
                rstd(k, 1, "ve3")
            normalize(B - 2, 0)
            rstd(PAIRS - 1, 0, "ve")
            rstd(PAIRS - 1, 1, "ve3")

        @block.scalar
        def _(act):
            act.dma_start(w_self[:, 1, :], sWk).then_inc(wkq_landed, 16)
            act.dma_start(w_self[:, 0, :], sWq).then_inc(wkq_landed, 16)
            act.dma_start(proj_sb[:], proj.rearrange("(g h) m d -> (h m) g d", g=G)).then_inc(proj_landed, 16)
            act.dma_start(wq_nat[:], xWq).then_inc(xqk_landed, 16)
            act.dma_start(wk_nat[:], xWk).then_inc(xqk_landed, 16)

            def evacuate(dst, name, src, step=None, scale=1.0):
                after(act, "pe", name)
                done("act", act.activation(dst, src, ACT.Copy, scale=scale), step or name)

            def bank(name):
                return banks[FILL_AT[name] % len(banks)]

            evacuate(projT[:], "projT", bank("projT"))
            for n, step in enumerate(("kT", "qT")):
                after(act, "dve", step)
                done("act", act.activation(kq_sq[:, n], kq_scaled[:, n], ACT.Square), f"square{n}")

            def exp_features(n, j):
                after(act, "dve", ("xw", (n, j)))
                done("act", act.activation(phi[:, n, j], phi[:, n, j], ACT.Exp), ("exp", (n, j)))

            exp_features(0, 0)
            evacuate(wT_self[:, 2:4], "wT_vo", bank("wT_vo")[:, 0:256].rearrange("p (n d) -> p n d", n=2))
            exp_features(1, 0)
            after(act, "pool", ("ones", 1))
            for par in range(2):
                rows = slice(SLOT * par, SLOT * par + S)
                src = bank("v").rearrange("p (j g c) -> p j g c", j=PAIRS, g=G)[rows]
                evacuate(v_masked[rows, :, par, :, 0:HG * DK], "v", src, "v" if par else "v0")

            def weight_copy(w, i):
                dst = {"q": wqT, "k": wkT, "v": wvT}[w]
                width = D if w == "q" else C
                src = bank(("wT", (w, i)))[:, 0:4 * width].rearrange("p (n c) -> p n c", n=4)
                evacuate(dst[:, 4 * i:4 * i + 4, :], ("wT", (w, i)), src)

            def qk_copy(i, par):
                dst = wqk[:, 8 * i:8 * i + 8, :].rearrange("p (n two) c -> p two n c", two=2)[:, par]
                src = bank(("wqk", (i, par)))[:, 0:4 * C].rearrange("p (n c) -> p n c", n=4)
                evacuate(dst, ("wqk", (i, par)), src, scale=float(XD) ** -0.5)

            def vo_copy(i, par):
                dst = wvo[:, 8 * i:8 * i + 8, :].rearrange("p (n two) d -> p two n d", two=2)[:, par]
                src = bank(("wvo", (i, par)))[0:C, :].rearrange("p (n d) -> p n d", n=4)
                evacuate(dst, ("wvo", (i, par)), src)

            def context_hi(b, par, slot, unit):
                act.wait_ge(mx_filled, slot + 1)
                act.activation(ct_hi[par][0:C, TW * unit:TW * unit + TW], mx[unit % 2][0:C, 0:TW],
                               ACT.Copy).then_inc(cthi_ready, 1)

            def context_rows_hi(b, par, landed):
                act.wait_ge(ctx_landed[par], 16 * landed)
                wait(act, pv_done, KT * (b - 1))
                act.activation(cn_hi[par][:, :, 0:C], ctx_nat[:, par], ACT.Copy).then_inc(nathi_ready, 1)

            def collect(b):
                act.wait_ge(pv_done, KT * (b + 1))
                act.wait_ge(unorm_ready, b + 1)
                for half in range(2):
                    act.activation(u[:, QH * half:QH * half + QH], acc[0:C + 1, half, 0:QH], ACT.Copy).then_inc(u_ready, 1)

            def tanh(pair, slot, at):
                act.wait_ge(mx_filled, slot + 1)
                act.activation(tanh_g[:], mx[at % 2][:, 0:HID], ACT.Tanh, scale=0.5).then_inc(tanh_ready, 1)

            def work(b, par, base, prep, pair, landed):
                plan = ring_plan(prep, pair is not None)
                number = slots(plan)
                for t in range(KT):
                    g = KT * b + t
                    if (t, 0) in plan and plan[(t, 0)][0] == "transpose":
                        context_hi(b + 1, 1 - par, base + number[(t, 0)], plan[(t, 0)][1])
                    if (t, 0) in plan and plan[(t, 0)][0] == "gate":
                        tanh(pair, base + number[(t, 0)], number[(t, 0)])
                    act.wait_ge(scores_ready, g + 1)
                    wait(act, plo_ready, g - 1)
                    act.activation(p_full[t % 2][:].rearrange("k (s q) -> k s q", s=2), sc[t % 2][0:KP, :, 0:QH],
                                   ACT.Exp)
                    if (t, 2) in plan and plan[(t, 2)][0] == "transpose":
                        context_hi(b + 1, 1 - par, base + number[(t, 2)], plan[(t, 2)][1])
                    wait(act, pv_done, g - 2)
                    act.activation(p_hi[t % 3][:].rearrange("k (s q) -> k s q", s=2), sc[t % 2][0:KP, :, 0:QH],
                                   ACT.Exp).then_inc(phi_ready, 1)
                    if t == 1 and not (isinstance(b, int) and b == 0):
                        collect(b - 1)
                    if t == 4 and prep:
                        context_rows_hi(b + 1, 1 - par, landed)

            def phiq_copy(j):
                after(act, "pe", ("phiqT", j))
                done("act", act.activation(phiqT[:, j], bank(("phiqT", j)).rearrange("p (g s) -> p g s", g=G), ACT.Copy,
                                           bias=SELF_EPS), ("phiqT", j))

            def merged_copy(j):
                evacuate(mergedT[:, j], ("mergedT", j), bank(("mergedT", j))[:, 0:128])

            def x1_hi(j):
                first = 1 if j == 0 else 0
                src = bank(("x1T", j))[:, 0:128].rearrange("p (b s) -> p b s", b=2)[:, first:, 0:S]
                evacuate(x1T_hi[:, 2 * j - 1 + first:2 * j + 1], ("x1T", j), src, ("x1T_hi", j))

            weight_copy("q", 0)
            exp_features(0, 1)
            weight_copy("k", 0)
            phiq_copy(0)
            exp_features(1, 1)
            qk_copy(0, 0)
            exp_features(0, 2)
            weight_copy("q", 1)
            merged_copy(0)
            qk_copy(0, 1)
            phiq_copy(1)
            exp_features(1, 2)
            weight_copy("k", 1)
            exp_features(0, 3)
            qk_copy(1, 0)
            qk_copy(1, 1)
            exp_features(1, 3)
            after(act, "dve", "x1T_first")
            x1_hi(0)
            context_hi(0, 0, 0, 0)
            context_hi(0, 0, 1, 1)
            merged_copy(1)
            phiq_copy(2)
            half = [bank(("q0", i))[0:C, :].rearrange("c (h s) -> c h s", s=SLOT)[:, :, 0:S] for i in range(2)]
            evacuate(q_hi[0][0:C, 0:QH].rearrange("c (h i) -> c h i", i=S), ("q0", 0), half[0], "q0_hi0")
            evacuate(q_all[:, 0, 0:QH].rearrange("c (h i) -> c h i", i=S), ("q0", 0), half[0])
            context_hi(0, 0, 2, 2)
            context_hi(0, 0, 3, 3)
            after(act, "dve", "q0_hi1")
            evacuate(q_all[:, 0, QH:].rearrange("c (h i) -> c h i", i=S), ("q0", 1), half[1])
            phiq_copy(3)
            weight_copy("v", 0)
            merged_copy(2)
            weight_copy("v", 1)
            context_rows_hi(0, 0, 1)
            merged_copy(3)
            for n in HEADS4:
                vo_copy(*n)
            for j in PR[1:]:
                x1_hi(j)
            for i in range(3):
                src = bank(("ffnT", i))[:, 0:HID].rearrange("p (c n) -> p c n", c=HC)
                evacuate(ffnT[:, i], ("ffnT", i), src)
            for h in range(H):
                src = bank(("qk", h))[0:C, 0:(B - 1) * S].rearrange("c (b s) -> c b s", b=B - 1)
                evacuate(q_all[:].rearrange("c b (h i) -> c b h i", h=H)[:, 1:B, h, :], ("qk", h), src)
            sequence_loop(act, work)
            collect(B - 1)
            tanh(PAIRS - 1, LAST_BASE + FINAL.index("gate"), FINAL.index("gate"))
            act.wait_ge(out_steps, out_step(PAIRS - 1, "x3"))
            act.dma_start(out.rearrange("(j p) i d -> p i j d", p=2)[1, :, PAIRS - 1],
                          x3[SLOT:SLOT + S, PAIRS - 1, :]).then_inc(stored, 16)

        @block.vector
        def _(dve):
            def bank(name):
                return banks[FILL_AT[name] % len(banks)]

            after(dve, "pe", "xT")
            done("dve", dve.tensor_copy(xT[:], bank("xT")), "xT")
            after(dve, "pe", "wT_kq")
            done("dve", dve.tensor_copy(wT_self[:, 0:2], bank("wT_kq")[:, 0:256].rearrange("p (n d) -> p n d", n=2)),
                 "wT_kq")
            for n, name in enumerate(("kT", "qT")):
                after(dve, "pe", name)
                done("dve", dve.tensor_scalar(kq_scaled[:, n], bank(name), float(DK) ** -0.5, None, ALU.mult), name)

            def context_lo(b, par, slot, unit):
                dve.wait_ge(mx_filled, slot + 1)
                dve.wait_ge(cthi_ready, TU * b + unit + 1)
                cols = slice(TW * unit, TW * unit + TW)
                dve.tensor_tensor(ct_lo[par][:, cols], mx[unit % 2][0:C, 0:TW], ct_hi[par][0:C, cols].bitcast(F32),
                                  ALU.subtract).then_inc(mx_freed, 1)

            def feature_max(n, j):
                name = ("xw", (n, j))
                after(dve, "pe", name)
                xw = bank(name).rearrange("p (h m) -> p h m", h=H)
                done("dve", dve.tensor_reduce(feat_max[:, n, j], xw, AX.X, ALU.max), ("fmax", (n, j)))

            def feature_shift(n, j):
                name = ("xw", (n, j))
                xw = bank(name).rearrange("p (h m) -> p h m", h=H)
                after(dve, "dve", ("fmax", (n, j)))
                done("dve", dve.tensor_tensor(feat_shift[:, n, j], half_sq[:, n, j], feat_max[:, n, j], ALU.add),
                     ("shift", (n, j)))
                after(dve, "dve", ("shift", (n, j)))
                done("dve", dve.tensor_tensor(phi[:, n, j], xw,
                                              feat_shift[:, n, j].unsqueeze(2).broadcast_to([128, H, M]),
                                              ALU.subtract), name)

            def feature(n, j):
                feature_max(n, j)
                if j == 0:
                    after(dve, "pe", ("norm", n))
                    done("dve", dve.tensor_copy(half_sq[:, n], bank(("norm", n))[:, 0:PAIRS * H].rearrange(
                        "p (j h) -> p j h", j=PAIRS)), ("norm", n))
                    after(dve, "dve", ("norm", n))
                feature_shift(n, j)

            def mask_kv(j):
                after(dve, "pe", ("kv", j))
                src = bank(("kv", j))[:, 0:G * 2 * KVW].rearrange("p (n c) -> p n c", c=KVW)
                done("dve", dve.tensor_tensor(kv[:, j].rearrange("p g s c -> p (g s) c"), src,
                                              block_mask[:].unsqueeze(1).broadcast_to([128, G * 2, KVW]), ALU.mult),
                     ("kv", j))

            def self_attention(j):
                after(dve, "pe", ("num", j))
                num = bank(("num", j))[:, 0:G * 2 * KVW].rearrange("p (g s c) -> p g s c", g=G, s=2)
                for par in range(2):
                    rows = slice(SLOT * par, SLOT * par + SLOT)
                    done("dve", dve.tensor_scalar(den[rows, j], num[rows, :, par, HG * DK:], float(M) * SELF_EPS, None,
                                                  ALU.add), ("den" if par else "den0", j))
                after(dve, "dve", ("den", j))
                done("dve", dve.reciprocal(rden[:, j], den[:, j]), ("rden", j))
                after(dve, "dve", ("rden", j))
                for par in range(2):
                    rows = slice(SLOT * par, SLOT * par + SLOT)
                    done("dve", dve.tensor_tensor(
                        merged[rows, j].rearrange("p (g h d) -> p g h d", g=G, h=HG),
                        num[rows, :, par, 0:HG * DK].rearrange("p g (h d) -> p g h d", h=HG),
                        rden[rows, j].unsqueeze(3).broadcast_to([SLOT, G, HG, DK]), ALU.mult),
                        ("num" if par else "num0", j))

            def residual(j):
                after(dve, "pe", ("self", j))
                after(dve, "pool", "xbias")
                done("dve", dve.tensor_tensor(y1[:, j], bank(("self", j))[:, 0:D], x_sb[:, j], ALU.add), ("self", j))
                after(dve, "dve", ("self", j))
                done("dve", dve.bn_stats(stats1[:, j], y1[:, j]), ("stats", j))
                after(dve, "dve", ("stats", j))
                done("dve", dve.bn_aggr(mv1[:, j], stats1[:, j]), ("aggr", j))

            def layer_norm(j):
                done("dve", dve.tensor_scalar(x1[:, j], y1[:, j], mv1[:, j, 0:1], rstd1[:, j:j + 1], ALU.subtract,
                                              ALU.mult), ("x1", j))

            def x1_lo(j):
                first = 1 if j == 0 else 0
                rows = slice(2 * j - 1 + first, 2 * j + 1)
                src = bank(("x1T", j))[:, 0:128].rearrange("p (b s) -> p b s", b=2)[:, first:, 0:S]
                after(dve, "pe", ("x1T", j))
                after(dve, "act", ("x1T_hi", j))
                done("dve", dve.tensor_tensor(x1T_lo[:, rows], src, x1T_hi[:, rows].bitcast(F32), ALU.subtract), ("x1T", j))

            feature(0, 0)
            feature(1, 0)
            feature(0, 1)
            feature(1, 1)
            after(dve, "pool", ("mask", HG - 1))
            mask_kv(0)
            feature(0, 2)
            self_attention(0)
            feature(1, 2)
            mask_kv(1)
            residual(0)
            after(dve, "dve", ("aggr", 0))
            done("dve", dve.tensor_scalar(ve1[:, 0:1], mv1[:, 0:1, 1], LN_EPS, None, ALU.add), "ve0")
            feature(0, 3)
            after(dve, "pool", "rstd0")
            layer_norm(0)
            self_attention(1)
            feature(1, 3)
            after(dve, "pe", ("x1T", 0))
            done("dve", dve.tensor_copy(x1T[:], bank(("x1T", 0))[:, 0:SLOT]), "x1T_first")
            mask_kv(2)
            after(dve, "act", ("wqk", HEADS4[-1]))
            done("dve", dve.tensor_copy(wqk_hi[:], wqk[:]), "wqk_hi")
            residual(1)
            context_lo(0, 0, 0, 0)
            x1_lo(0)
            context_lo(0, 0, 1, 1)
            after(dve, "pe", ("q0", 1))
            done("dve", dve.tensor_copy(q_hi[0][0:C, QH:].rearrange("c (h i) -> c h i", i=S),
                                        bank(("q0", 1))[0:C, :].rearrange("c (h s) -> c h s", s=SLOT)[:, :, 0:S]), "q0_hi1")
            after(dve, "dve", "q0_hi1")
            after(dve, "act", "q0_hi0")
            dve.sem_inc(qhi_ready, 1)
            context_lo(0, 0, 2, 2)
            self_attention(2)
            context_lo(0, 0, 3, 3)
            mask_kv(3)

            def chunk_max(slot, at, j, c):
                dve.wait_ge(mx_filled, slot + 1)
                dve.tensor_reduce(max_part[:, j, c:c + 1], mx[at % 2][:, 0:KC], AX.X, ALU.max).then_inc(mx_freed, 1)

            def join_maxima(b, slot):
                dve.wait_ge(mx_freed, slot)
                dve.tensor_reduce(max_neg[:], max_part[:], AX.X, ALU.max, negate=True).then_inc(maxneg_ready, 1)

            def copy_maxima(b, slot, at):
                dve.wait_ge(mx_filled, slot + 1)
                dve.tensor_copy(max_row[:], mx[at % 2][0:QT, 0:128]).then_inc(mx_freed, 1)
                dve.wait_ge(mx_freed, slot + 1)
                dve.sem_inc(maxrow_ready, 1)

            def exp_lo(g, t):
                dve.wait_ge(phi_ready, g + 1)
                wait(dve, pv_done, g - 2)
                dve.tensor_tensor(p_lo[t % 3][:], p_full[t % 2][:], p_hi[t % 3][:].bitcast(F32),
                                  ALU.subtract).then_inc(plo_ready, 1)

            def reciprocals(b):
                dve.wait_ge(sums_landed, 16 * (b + 1))
                dve.reciprocal(rsums[:], sums[:]).then_inc(rsums_ready, 1)

            def step(pair, ins, name):
                ins.then_inc(out_steps, 1)
                dve.wait_ge(out_steps, out_step(pair, name))

            def layer_norm_stats(pair, src, tail):
                dve.bn_stats(stats2[:], src).then_inc(out_steps, 1)
                dve.wait_ge(out_steps, out_step(pair, "stats" + tail))
                dve.sem_inc(dve_waited, 1)
                step(pair, dve.bn_aggr(mv2[:], stats2[:]), "aggr" + tail)
                step(pair, dve.tensor_scalar(ve2[:], mv2[:, 1:2], LN_EPS, None, ALU.add), "ve" + tail)

            def output(what, pair, slot, at):
                src = mx[at % 2]
                dve.wait_ge(mx_filled, slot + 1)
                if what == "out":
                    step(pair, dve.tensor_tensor(y2[:], src[:, 0:D], x1b[:, pair, :], ALU.add), "y2")
                    dve.sem_inc(mx_freed, 1)
                    layer_norm_stats(pair, y2[:], "")
                if what == "x2T":
                    step(pair, dve.tensor_copy(x2T[:], src[:, 0:128]), "x2T")
                    dve.sem_inc(mx_freed, 1)
                if what == "gate":
                    dve.wait_ge(tanh_ready, pair + 1)
                    step(pair, dve.scalar_tensor_tensor(out=silu_g[:], in0=tanh_g[:], scalar=1.0, in1=src[:, 0:HID],
                                                        op0=ALU.add, op1=ALU.mult), "silu")
                    dve.sem_inc(mx_freed, 1)
                if what == "up":
                    step(pair, dve.scalar_tensor_tensor(out=hidT[:].rearrange("p c s -> p (c s)"), in0=silu_g[:],
                                                        scalar=0.5, in1=src[:, 0:HID], op0=ALU.mult, op1=ALU.mult), "hid")
                    dve.sem_inc(mx_freed, 1)
                if what == "down":
                    step(pair, dve.tensor_tensor(y2[:], src[:, 0:D], x2[:], ALU.add), "y3")
                    dve.sem_inc(mx_freed, 2)
                    layer_norm_stats(pair, y2[:], "3")

            def finish_norm(pair, dst, n, name):
                dve.wait_ge(rstd_ready, 2 * pair + n)
                step(pair, dve.tensor_scalar(dst, y2[:], mv2[:, 0:1], rstd2[:], ALU.subtract, ALU.mult), name)

            def queries_hi(b, par):
                wait(dve, scores_ready, KT * (b - 1))
                dve.tensor_copy(q_hi[par][0:C, :], q_all[:, b, :]).then_inc(qhi_ready, 1)

            def work(b, par, base, prep, pair, landed):
                plan = ring_plan(prep, pair is not None)
                number = slots(plan)
                if prep:
                    if isinstance(b, int):
                        after(dve, "act", ("qk", H - 1))
                    queries_hi(b + 1, 1 - par)
                for t in range(KT):
                    for p in range(4):
                        if p == 2 and not (isinstance(b, int) and b == 0 and t == 0):
                            exp_lo(KT * b + t - 1, (t - 1) % KT)
                        if (t, p) not in plan:
                            continue
                        (kind, what), at = plan[(t, p)], number[(t, p)]
                        if kind == "transpose":
                            context_lo(b + 1, 1 - par, base + at, what)
                        elif kind == "max":
                            chunk_max(base + at, at, *what)
                            if what == MAXES[-1]:
                                join_maxima(b + 1, base + at + 1)
                        elif kind == "maxrow":
                            copy_maxima(b + 1, base + at, at)
                        else:
                            output(kind, pair, base + at, at)
                    if t == 3 and not (isinstance(b, int) and b == 0):
                        reciprocals(b - 1)
                    if t == 8 and pair is not None:
                        finish_norm(pair, x2[:], 1, "x2")
                if pair is not None:
                    finish_norm(pair, x3[:, pair, :], 2, "x3")

            for n, (j, c) in enumerate(MAXES):
                chunk_max(TU + n, TU + n, j, c)
                if n == 0:
                    self_attention(3)
                if n == 1:
                    residual(2)
                if n == 2:
                    residual(3)
                    after(dve, "dve", ("aggr", PAIRS - 1))
                    done("dve", dve.tensor_scalar(ve1[:, 1:], mv1[:, 1:, 1], LN_EPS, None, ALU.add), "ve")
                if n == 4:
                    after(dve, "pool", "rstd")
                    for i in PR[1:]:
                        layer_norm(i)
                if n == 5:
                    for i in PR[1:]:
                        x1_lo(i)
            join_maxima(0, PREP_SLOTS - 1)
            done("dve", dve.tensor_tensor(x1b[:], x1[:], xbo_sb[:].unsqueeze(1).broadcast_to([128, PAIRS, D]),
                                          ALU.add), "x1b")
            copy_maxima(0, PREP_SLOTS - 1, PREP_SLOTS - 1)
            sequence_loop(dve, work)
            exp_lo(KT * B - 1, KT - 1)
            chunks = Q // SUM_P // 2
            for half in range(2):
                cols = slice(chunks * half, chunks * half + chunks)
                dve.wait_ge(sums_turned, half + 1)
                turned = sc[0][0:SUM_P, half, 0:(C + 1) * chunks].rearrange("p (n c) -> p n c", n=chunks)
                dve.reciprocal(last_recip[:, cols], turned[:, :, C]).then_inc(recip_ready, 1)
            for half in range(2):
                dve.wait_ge(recip_spread, half + 1)
                dve.tensor_tensor(u_norm[:, 8 * half:8 * half + 8, 1, 0:S],
                                  u[0:C, QH * half:QH * half + QH].rearrange("c (h i) -> c h i", i=S),
                                  acc[0:C, half, 0:QH].rearrange("c (h i) -> c h i", i=S), ALU.mult).then_inc(last_norm, 1)
            for n, what in enumerate(FINAL):
                output(what, PAIRS - 1, LAST_BASE + n, n)
                if what == "out":
                    finish_norm(PAIRS - 1, x2[:], 1, "x2")
            finish_norm(PAIRS - 1, x3[:, PAIRS - 1, :], 2, "x3")

        @block.tensor
        def _(pe):
            def fill(name):
                n = FILL_AT[name]
                if n >= len(banks):
                    before, engine = FILLS[n - len(banks)]
                    after(pe, engine, before)
                return banks[n % len(banks)]

            def mm(dst, lhsT, rhs, start=True, stop=True):
                return pe.matmul(dst, lhsT, rhs, start=start, stop=stop, skip_group_check=True)

            after(pe, "pool", "ident")
            pe.wait_ge(x_landed, 32)
            dst = fill("xT")
            for j in PR:
                last = pe.transpose(dst[:, 128 * j:128 * j + 128], x_sb[:, j], ident[:])
            done("pe", last, "xT")
            def self_weights(name, first):
                dst = fill(name)
                for n in range(2):
                    last = pe.transpose(dst[:, 128 * n:128 * n + 128], w_self[:, first + n], ident[:])
                done("pe", last, name)

            pe.wait_ge(wkq_landed, 32)
            self_weights("wT_kq", 0)
            after(pe, "dve", "xT")
            after(pe, "dve", "wT_kq")
            done("pe", mm(fill("kT"), wT_self[:, 1], xT[:]), "kT")
            after(pe, "pool", ("wide", HG - 1))
            dst = fill("projT")
            for g in range(G):
                last = pe.transpose(dst[:, 128 * g:128 * g + 128], proj_wide[:, g].rearrange("p h d -> p (h d)"), ident[:])
            done("pe", last, "projT")
            done("pe", mm(fill("qT"), wT_self[:, 0], xT[:]), "qT")

            def random_features(n, j):
                after(pe, "act", "projT")
                after(pe, "dve", "qT" if n else "kT")
                done("pe", mm(fill(("xw", (n, j))), kq_scaled[:, n, 128 * j:128 * j + 128], projT[:]), ("xw", (n, j)))

            def weight_transposes(w, i):
                src = {"q": wq_nat, "k": wk_nat, "v": wv_nat}[w]
                width = D if w == "q" else C
                dst = fill(("wT", (w, i)))
                for n in range(4):
                    cols = slice(128 * (4 * i + n), 128 * (4 * i + n) + 128)
                    last = pe.transpose(dst[:, width * n:width * n + width], src[:, cols], ident[0:width, 0:width])
                done("pe", last, ("wT", (w, i)))

            def head_products(name, i, par, lhs, rhs, lhs_width, width):
                dst = fill((name, (i, par)))
                rows = slice(XD * par, XD * par + XD)
                for n in range(4):
                    last = mm(dst[0:lhs_width, width * n:width * n + width], lhs[rows, 4 * i + n, :],
                              rhs[rows, 4 * i + n, :])
                done("pe", last, (name, (i, par)))

            def half_norms(n):
                after(pe, "pool", "norm2")
                after(pe, "act", f"square{n}")
                dst = fill(("norm", n))
                for j in PR:
                    last = mm(dst[:, j * H:j * H + H], kq_sq[:, n, 128 * j:128 * j + 128], half_norm[:])
                done("pe", last, ("norm", n))

            random_features(0, 0)
            half_norms(0)
            random_features(1, 0)
            half_norms(1)
            pe.wait_ge(wvo_landed, 32)
            self_weights("wT_vo", 2)
            after(pe, "act", "wT_vo")
            dst = fill("v")
            for j in PR:
                last = mm(dst[:, 128 * j:128 * j + 128], xT[:, 128 * j:128 * j + 128], wT_self[:, 2])
            done("pe", last, "v")

            def ring(slot):
                wait(pe, mx_freed, slot - 1)

            def context_transposes(b, par, slot, unit, landed):
                ring(slot)
                pe.wait_ge(ctx_landed[par], 16 * landed)
                for n in range(KT // TU):
                    last = pe.transpose(mx[unit % 2][0:C, KP * n:KP * n + KP], ctx_nat[:, par, 3 * unit + n],
                                        ident[0:KP, 0:KP])
                last.then_inc(mx_filled, 1)

            def max_scores(b, par, slot, at, j, c):
                ring(slot)
                pe.wait_ge(qhi_ready, b + 1)
                pe.wait_ge(cthi_ready, TU * (b + 1))
                mm(mx[at % 2][:, 0:KC], q_hi[par][0:C, 128 * j:128 * j + 128],
                   ct_hi[par][0:C, KC * c:KC * c + KC]).then_inc(mx_filled, 1)

            def turn_maxima(b, slot, at):
                ring(slot)
                pe.wait_ge(maxneg_ready, b + 1)
                pe.transpose(mx[at % 2][0:QT, 0:128], max_neg[:], ident[:]).then_inc(mx_filled, 1)

            def scores(g, t, par, half):
                dst = sc[t % 2][0:KP, half, 0:QH]
                cols, keys = slice(QH * half, QH * half + QH), slice(KP * t, KP * t + KP)
                mm(dst, ct_hi[par][:, keys], q_hi[par][:, cols], True, False)
                mm(dst, ct_lo[par][:, keys], q_hi[par][0:C, cols], False, False)
                last = mm(dst, ct_hi[par][0:C, keys], q_lo[par][:, cols], False, True)
                if half:
                    last.then_inc(scores_ready, 1)

            def context_sum(t, par, half):
                dst = acc[0:C + 1, half, 0:QH]
                cols = slice(QH * half, QH * half + QH)
                mm(dst, cn_hi[par][:, t], p_hi[t % 3][:, cols], t == 0, False)
                mm(dst, cn_lo[par][:, t], p_hi[t % 3][:, cols], False, False)
                last = mm(dst, cn_hi[par][:, t], p_lo[t % 3][:, cols], False, t == KT - 1)
                if half:
                    last.then_inc(pv_done, 1)

            def output(what, pair, slot, at):
                ring(slot)
                dst = mx[at % 2]
                if what == "out":
                    last_pair = isinstance(pair, int) and pair == PAIRS - 1
                    pe.wait_ge(unorm_ready, 2 * pair + (2 if last_pair else 3))
                    for h in range(H):
                        if last_pair and h % 8 == 0:
                            pe.wait_ge(last_norm, h // 8 + 1)
                        last = mm(dst[:, 0:D], u_norm[:, h].rearrange("c p s -> c (p s)"), wvo[:, h], h == 0, h == H - 1)
                if what == "x2T":
                    pe.wait_ge(out_steps, out_step(pair, "x2"))
                    last = pe.transpose(dst[:, 0:128], x2[:], ident[:])
                if what in ("gate", "up"):
                    pe.wait_ge(out_steps, out_step(pair, "x2T"))
                    for c in range(HC):
                        last = mm(dst[:, 128 * c:128 * c + 128], ffnT[:, 0 if what == "gate" else 1, c], x2T[:])
                if what == "down":
                    pe.wait_ge(out_steps, out_step(pair, "hid"))
                    for c in range(HC):
                        last = mm(dst[:, 0:D], hidT[:, c], ffnT[:, 2, c], c == 0, c == HC - 1)
                last.then_inc(mx_filled, 2 if what == "down" else 1)

            def sum_step(b, t, par, part):
                if part == 0:
                    pe.wait_ge(plo_ready, KT * b + t + 1)
                    if t == 0:
                        pe.wait_ge(nat_ready, b + 1)
                if t == 0:
                    wait(pe, u_ready, 2 * b - 1 + part if not (isinstance(b, int) and b == 0) else 0)
                context_sum(t, par, part)

            def work(b, par, base, prep, pair, landed):
                plan = ring_plan(prep, pair is not None)
                number = slots(plan)

                def extra(t, p):
                    if (t, p) not in plan:
                        return
                    (kind, what), at = plan[(t, p)], number[(t, p)]
                    if kind == "transpose":
                        context_transposes(b + 1, 1 - par, base + at, what, landed)
                    elif kind == "max":
                        max_scores(b + 1, 1 - par, base + at, at, *what)
                    elif kind == "maxrow":
                        turn_maxima(b + 1, base + at, at)
                    else:
                        output(kind, pair, base + at, at)

                first = isinstance(b, int) and b == 0
                for t in range(KT):
                    extra(t, 0)
                    g = KT * b + t
                    if t == 0:
                        pe.wait_ge(maxrow_landed, 16 * (b + 1))
                        pe.wait_ge(qlo_ready, b + 1)
                    wait(pe, phi_ready, g - 1)
                    scores(g, t, par, 0)
                    extra(t, 1)
                    scores(g, t, par, 1)
                    extra(t, 2)
                    if t >= 2:
                        sum_step(b, t - 2, par, 0)
                    elif not first:
                        sum_step(b - 1, KT + t - 2, 1 - par, 0)
                    extra(t, 3)
                    if t >= 2:
                        sum_step(b, t - 2, par, 1)
                    elif not first:
                        sum_step(b - 1, KT + t - 2, 1 - par, 1)

            def transposed_context(unit):
                context_transposes(0, 0, unit, unit, 1)

            def products_qk(i, par):
                head_products("wqk", i, par, wqT, wkT, D, C)

            def products_vo(i, par):
                head_products("wvo", i, par, wvT, wo_nat, C, D)

            def key_values(j):
                after(pe, "pool", ("eps", j))
                dst = fill(("kv", j))
                for g in range(G):
                    last = mm(dst[:, 2 * KVW * g:2 * KVW * (g + 1)].rearrange("p (s c) -> p s c", s=2),
                              phi[:, 0, j, HG * g:HG * g + HG, :].rearrange("p h m -> p (h m)"), v_masked[:, j, :, g, :])
                done("pe", last, ("kv", j))

            def turn_phiq(j):
                after(pe, "act", ("exp", (1, j)))
                dst = fill(("phiqT", j))
                for g in range(G):
                    last = pe.transpose(dst[:, 128 * g:128 * g + 128],
                                        phi[:, 1, j, HG * g:HG * g + HG, :].rearrange("p h m -> p (h m)"), ident[:])
                done("pe", last, ("phiqT", j))

            def numerators(j):
                after(pe, "act", ("phiqT", j))
                after(pe, "dve", ("kv", j))
                dst = fill(("num", j))
                for g in range(G):
                    last = mm(dst[:, 2 * KVW * g:2 * KVW * (g + 1)], phiqT[:, j, g, :],
                              kv[:, j, g].rearrange("p s c -> p (s c)"))
                done("pe", last, ("num", j))

            def x1_transpose(j):
                after(pe, "dve", ("x1", j))
                done("pe", pe.transpose(fill(("x1T", j))[:, 0:128], x1[:, j], ident[:]), ("x1T", j))

            def turn_merged(j):
                after(pe, "dve", ("num", j))
                done("pe", pe.transpose(fill(("mergedT", j))[:, 0:128], merged[:, j], ident[:]), ("mergedT", j))

            def project(j):
                after(pe, "act", ("mergedT", j))
                done("pe", mm(fill(("self", j))[:, 0:D], mergedT[:, j], wT_self[:, 3]), ("self", j))

            def first_queries():
                after(pe, "dve", "x1T_first")
                after(pe, "act", ("wqk", HEADS4[-1]))
                for i in range(2):
                    dst = fill(("q0", i))
                    for h in range(8):
                        last = mm(dst[0:C, SLOT * h:SLOT * h + SLOT], wqk[:, 8 * i + h], x1T[:])
                    done("pe", last, ("q0", i))

            def first_maxima(n):
                max_scores(0, 0, TU + n, TU + n, *MAXES[n])

            def ffn_transpose(i):
                after(pe, "pool", ("ffn", i))
                dst = fill(("ffnT", i))
                for c in range(HC):
                    last = pe.transpose(dst[:, 128 * c:128 * c + 128], ffn_nat[:, i, c], ident[:])
                done("pe", last, ("ffnT", i))

            random_features(0, 1)
            pe.wait_ge(xqk_landed, 32)
            weight_transposes("q", 0)
            random_features(1, 1)
            after(pe, "act", "v")
            key_values(0)
            weight_transposes("k", 0)
            turn_phiq(0)
            random_features(0, 2)
            after(pe, "act", ("wT", ("k", 0)))
            products_qk(0, 0)
            numerators(0)
            random_features(1, 2)
            weight_transposes("q", 1)
            turn_merged(0)
            products_qk(0, 1)
            key_values(1)
            turn_phiq(1)
            project(0)
            random_features(0, 3)
            weight_transposes("k", 1)
            numerators(1)
            random_features(1, 3)
            after(pe, "act", ("wT", ("k", 1)))
            products_qk(1, 0)
            products_qk(1, 1)
            x1_transpose(0)
            key_values(2)
            transposed_context(0)
            transposed_context(1)
            turn_merged(1)
            project(1)
            turn_phiq(2)
            first_queries()
            transposed_context(2)
            numerators(2)
            transposed_context(3)
            key_values(3)
            turn_phiq(3)
            pe.wait_ge(xvo_landed, 32)
            weight_transposes("v", 0)
            turn_merged(2)
            after(pe, "pool", "ones0")
            first_maxima(0)
            numerators(3)
            project(2)
            first_maxima(1)
            weight_transposes("v", 1)
            turn_merged(3)
            after(pe, "act", ("wT", ("v", 1)))
            products_vo(0, 0)
            project(3)
            first_maxima(2)
            products_vo(0, 1)
            first_maxima(3)
            products_vo(1, 0)
            first_maxima(4)
            products_vo(1, 1)
            for j in PR[1:]:
                x1_transpose(j)
            for i in range(3):
                first_maxima(5 + i)
                ffn_transpose(i)
            after(pe, "dve", ("x1T", PAIRS - 1))
            after(pe, "pool", "wqk_lo")
            others_hi = x1T_hi[:].rearrange("p b s -> p (b s)")
            others_lo = x1T_lo[:].rearrange("p b s -> p (b s)")

            def other_queries(h):
                dst = fill(("qk", h))[0:C, 0:(B - 1) * S]
                mm(dst, wqk_hi[:, h], others_hi, True, False)
                mm(dst, wqk_lo[:, h], others_hi, False, False)
                done("pe", mm(dst, wqk_hi[:, h], others_lo, False, True), ("qk", h))

            late = 3
            begun, early = 8, H - late
            for n in range(len(MAXES) - begun):
                for h in range(early * n // (len(MAXES) - begun), early * (n + 1) // (len(MAXES) - begun)):
                    other_queries(h)
                first_maxima(begun + n)
            other_queries(H - late)
            turn_maxima(0, PREP_SLOTS - 1, PREP_SLOTS - 1)
            for h in range(H - late + 1, H):
                other_queries(h)
            after(pe, "act", ("qk", H - 1))

            sequence_loop(pe, work)
            for half in range(2):
                sum_step(B - 1, KT - 2, 1, half)
            tail_cols = [slice(QH * half, QH * half + QH) for half in range(2)]
            tail_dst = [acc[0:C + 1, half, 0:QH] for half in range(2)]
            t = KT - 1
            pe.wait_ge(phi_ready, KT * B)
            for half in range(2):
                mm(tail_dst[half], cn_hi[1][:, t], p_hi[t % 3][:, tail_cols[half]], False, False)
                mm(tail_dst[half], cn_lo[1][:, t], p_hi[t % 3][:, tail_cols[half]], False, False)
            pe.wait_ge(plo_ready, KT * B)
            for half in range(2):
                last = mm(tail_dst[half], cn_hi[1][:, t], p_lo[t % 3][:, tail_cols[half]], False, True)
            last.then_inc(pv_done, 1)
            chunks = Q // SUM_P // 2
            for half in range(2):
                pe.wait_ge(u_ready, 2 * B - 1 + half)
                for n in range(chunks):
                    at = SUM_P * (chunks * half + n)
                    last = pe.transpose(sc[0][0:SUM_P, half, (C + 1) * n:(C + 1) * (n + 1)], u[:, at:at + SUM_P],
                                        ident[0:C + 1, 0:C + 1])
                last.then_inc(sums_turned, 1)
            for half in range(2):
                pe.wait_ge(recip_ready, half + 1)
                for n in range(chunks):
                    column = last_recip[:, chunks * half + n:chunks * half + n + 1]
                    last = mm(acc[0:C, half, SUM_P * n:SUM_P * n + SUM_P], column.broadcast_to([SUM_P, C]),
                              ident[0:SUM_P, 0:SUM_P])
                last.then_inc(recip_spread, 1)
            for n, what in enumerate(FINAL):
                output(what, PAIRS - 1, LAST_BASE + n, n)


_INS = ['x', 'ctx_768', 'L0_attn_Wq', 'L0_attn_Wk', 'L0_attn_Wv', 'L0_attn_Wo', 'L0_attn_bo', 'L0_attn_proj',
        'L0_xattn_Wq', 'L0_xattn_Wk', 'L0_xattn_Wv', 'L0_xattn_Wo', 'L0_xattn_bo',
        'L0_ffn_w_gate', 'L0_ffn_w_up', 'L0_ffn_w_down']
_OUTS = [((B, S, D), 'float32')]


def kernel(**inputs):
    import numpy as _np
    import concourse.bacc as _bacc
    from concourse import mybir as _mybir
    from concourse.bass_utils import run_bass_kernel_spmd as _run

    nc = _bacc.Bacc("TRN2", target_bir_lowering=False, num_devices=1)
    arrays, args = {}, []
    for name in _INS:
        a = _np.ascontiguousarray(inputs[name])
        arrays[f"in_{name}_dram"] = a
        args.append(nc.dram_tensor(f"in_{name}_dram", a.shape, _mybir.dt.from_np(a.dtype), kind="ExternalInput").ap())
    for i, (shape, dtype) in enumerate(_OUTS):
        dt = _mybir.dt.from_np(_np.dtype(dtype))
        args.append(nc.dram_tensor(f"out_{i}_dram", shape, dt, kind="ExternalOutput").ap())
    program(nc, *args)
    r = _run(nc, [arrays], core_ids=[0])
    got = tuple(r.results[0][f"out_{i}_dram"] for i in range(len(_OUTS)))
    return got[0]
```
